# Optimizing a Trainium2 kernel written in Bass

```python
import numpy as np
import jax
import jax.numpy as jnp

def _softmax(x, axis=-1):
    return jax.nn.softmax(x, axis=axis)

def _gelu(x):
    return jax.nn.gelu(x, approximate=True)

def _silu(x):
    return jax.nn.silu(x)

def _sigmoid(x):
    return jax.nn.sigmoid(x)

def _layernorm(x, axis=-1, eps=1e-05):
    m = jnp.mean(x, axis=axis, keepdims=True)
    v = jnp.var(x, axis=axis, keepdims=True)
    return (x - m) / jnp.sqrt(v + eps)

def _scatter_add(tgt, idx, src, axis=0):
    return tgt.at[idx].add(src)

def _segment_sum(src, seg, n):
    return jax.ops.segment_sum(src, seg, n)
kernel_name = 'mk_gnn_preln_d4_gnn_r32_5a5eee'

def setup_inputs(seed: int=0):
    np.random.seed(seed)
    _w = jnp.asarray

    def _rec_inputs():
        import jax
        import jax.numpy as jnp
        _gk = jax.random.key(seed)
        x = -0.0003713 + 1 * jax.random.normal(jax.random.fold_in(_gk, 1), (50000, 128), jnp.float32)
        src = jax.random.randint(jax.random.fold_in(_gk, 2), (50000,), 0, 50000, jnp.int32)
        dst = jnp.minimum((50000 * jax.random.uniform(jax.random.fold_in(_gk, 3), (50000,)) ** 2.0).astype(jnp.int32), 49999)
        _o = jnp.argsort(dst, stable=True)
        src = src[_o]
        dst = dst[_o]
        edge_weight = jax.random.uniform(jax.random.fold_in(_gk, 13), (50000,), jnp.float32, 0.0, 0.999998)
        return (x, src, dst, edge_weight)
    x, src, dst, edge_weight = _rec_inputs()

    def _L0_gnn_setup():
        import jax, jax.numpy as jnp
        import numpy as np
        N_NODES = 3125
        N_EDGES = 50000
        IN_FEATS = 128
        H_FEATS = 128

        def _degree_norms(src, dst, n_nodes):
            ones = jnp.ones(src.shape[0], dtype=jnp.float32)
            deg_out = jax.ops.segment_sum(ones, src, num_segments=n_nodes)
            deg_in = jax.ops.segment_sum(ones, dst, num_segments=n_nodes)
            norm_src = jax.lax.rsqrt(jnp.maximum(deg_out, 1.0))
            norm_dst = jax.lax.rsqrt(jnp.maximum(deg_in, 1.0))
            return (norm_src, norm_dst)

        def _graph_conv(x, W, b, src, dst, norm_src, norm_dst, n_nodes):
            h = x * norm_src[:, None] @ W
            msgs = jnp.take(h, src, axis=0)
            agg = jax.ops.segment_sum(msgs, dst, num_segments=n_nodes)
            return agg * norm_dst[:, None] + b
        key = jax.random.key(seed)
        k1, k2, k3, k4, k5 = jax.random.split(key, 5)
        features = jax.random.normal(k1, (N_NODES, IN_FEATS), dtype=jnp.float32)
        src = jax.random.randint(k2, (N_EDGES,), 0, N_NODES, dtype=jnp.int32)
        dst = jax.random.randint(k3, (N_EDGES,), 0, N_NODES, dtype=jnp.int32)
        W1 = jax.random.normal(k4, (IN_FEATS, H_FEATS), dtype=jnp.float32) / np.sqrt(IN_FEATS)
        W2 = jax.random.normal(k5, (H_FEATS, H_FEATS), dtype=jnp.float32) / np.sqrt(H_FEATS)
        b1 = jnp.zeros((H_FEATS,), dtype=jnp.float32)
        b2 = jnp.zeros((H_FEATS,), dtype=jnp.float32)
        return {'features': features, 'src': src, 'dst': dst, 'W1': W1, 'b1': b1, 'W2': W2, 'b2': b2}
    _L0_gnn_all = _L0_gnn_setup()
    _L0_gnn_in = {k: v for k, v in _L0_gnn_all.items() if k in ('W1', 'b1', 'W2', 'b2')}
    del _L0_gnn_all

    def _L1_gnn_setup():
        import jax, jax.numpy as jnp
        import numpy as np
        N_NODES = 50000
        N_EDGES = 25000
        IN_FEATS = 128
        N_CLASSES = 128
        key = jax.random.key(seed)
        k1, k2, k3, k4, k5 = jax.random.split(key, 5)
        x = jax.random.normal(k1, (N_NODES, IN_FEATS), dtype=jnp.float32)
        W = jax.random.normal(k2, (N_CLASSES, 2 * IN_FEATS), dtype=jnp.float32) * 0.05
        b = jax.random.normal(k3, (N_CLASSES,), dtype=jnp.float32) * 0.05
        src = jax.random.randint(k4, (N_EDGES,), 0, N_NODES, dtype=jnp.int64)
        dst = jax.random.randint(k5, (N_EDGES,), 0, N_NODES, dtype=jnp.int64)
        return {'x': x, 'W': W, 'b': b, 'src': src, 'dst': dst}
    _L1_gnn_all = _L1_gnn_setup()
    _L1_gnn_in = {k: v for k, v in _L1_gnn_all.items() if k in ('W', 'b')}
    del _L1_gnn_all

    def _L2_gnn_setup():
        import jax, jax.numpy as jnp
        import numpy as np
        N_NODES = 50000
        N_EDGES = 25000
        IN_FEATS, HID_FEATS, OUT_FEATS = (128, 256, 128)
        key = jax.random.key(seed)
        ks = jax.random.split(key, 8)
        x = jax.random.normal(ks[0], (N_NODES, IN_FEATS), dtype=jnp.float32)
        src = jax.random.randint(ks[1], (N_EDGES,), 0, N_NODES)
        dst = jax.random.randint(ks[2], (N_EDGES,), 0, N_NODES)
        W_self1 = jax.random.normal(ks[3], (IN_FEATS, HID_FEATS), dtype=jnp.float32) / np.sqrt(IN_FEATS)
        W_neigh1 = jax.random.normal(ks[4], (IN_FEATS, HID_FEATS), dtype=jnp.float32) / np.sqrt(IN_FEATS)
        b1 = jnp.zeros((HID_FEATS,), dtype=jnp.float32)
        W_self2 = jax.random.normal(ks[5], (HID_FEATS, OUT_FEATS), dtype=jnp.float32) / np.sqrt(HID_FEATS)
        W_neigh2 = jax.random.normal(ks[6], (HID_FEATS, OUT_FEATS), dtype=jnp.float32) / np.sqrt(HID_FEATS)
        b2 = jnp.zeros((OUT_FEATS,), dtype=jnp.float32)
        return {'x': x, 'src': src, 'dst': dst, 'W_self1': W_self1, 'W_neigh1': W_neigh1, 'b1': b1, 'W_self2': W_self2, 'W_neigh2': W_neigh2, 'b2': b2}
    _L2_gnn_all = _L2_gnn_setup()
    _L2_gnn_in = {k: v for k, v in _L2_gnn_all.items() if k in ('W_self1', 'W_neigh1', 'b1', 'W_self2', 'W_neigh2', 'b2')}
    del _L2_gnn_all

    def _L3_gnn_setup():
        import jax, jax.numpy as jnp
        import numpy as np
        HID = 128
        N_NODES = 50000
        N_EDGES = 18750

        def _layernorm(x, gamma, beta, eps=1e-05):
            mu = jnp.mean(x, axis=-1, keepdims=True)
            var = jnp.var(x, axis=-1, keepdims=True)
            return (x - mu) * jax.lax.rsqrt(var + eps) * gamma + beta
        key = jax.random.key(seed)
        ks = jax.random.split(key, 12)
        d = HID
        s = lambda fan_in: 1.0 / np.sqrt(fan_in)
        return {'hidden': jax.random.normal(ks[0], (N_NODES, d), dtype=jnp.float32), 'edge_index': jax.random.randint(ks[1], (2, N_EDGES), 0, N_NODES, dtype=jnp.int32), 'edge_weight': jax.random.uniform(ks[2], (N_EDGES,), dtype=jnp.float32), 'We1': jax.random.uniform(ks[3], (2 * d + 1, d), jnp.float32, -s(2 * d + 1), s(2 * d + 1)), 'be1': jnp.zeros((d,), jnp.float32), 'We2': jax.random.uniform(ks[4], (d, d), jnp.float32, -s(d), s(d)), 'be2': jnp.zeros((d,), jnp.float32), 'Wu1': jax.random.uniform(ks[5], (2 * d, d), jnp.float32, -s(2 * d), s(2 * d)), 'bu1': jnp.zeros((d,), jnp.float32), 'Wu2': jax.random.uniform(ks[6], (d, d), jnp.float32, -s(d), s(d)), 'bu2': jnp.zeros((d,), jnp.float32), 'gamma': jnp.ones((d,), jnp.float32), 'beta': jnp.zeros((d,), jnp.float32)}
    _L3_gnn_all = _L3_gnn_setup()
    _L3_gnn_in = {k: v for k, v in _L3_gnn_all.items() if k in ('We1', 'be1', 'We2', 'be2', 'Wu1', 'bu1', 'Wu2', 'bu2', 'gamma', 'beta')}
    del _L3_gnn_all
    return {'x': x, 'src': src, 'dst': dst, 'edge_weight': edge_weight, 'L0_gnn_W1': _L0_gnn_in['W1'], 'L0_gnn_b1': _L0_gnn_in['b1'], 'L0_gnn_W2': _L0_gnn_in['W2'], 'L0_gnn_b2': _L0_gnn_in['b2'], 'L1_gnn_W': _L1_gnn_in['W'], 'L1_gnn_b': _L1_gnn_in['b'], 'L2_gnn_W_self1': _L2_gnn_in['W_self1'], 'L2_gnn_W_neigh1': _L2_gnn_in['W_neigh1'], 'L2_gnn_b1': _L2_gnn_in['b1'], 'L2_gnn_W_self2': _L2_gnn_in['W_self2'], 'L2_gnn_W_neigh2': _L2_gnn_in['W_neigh2'], 'L2_gnn_b2': _L2_gnn_in['b2'], 'L3_gnn_We1': _L3_gnn_in['We1'], 'L3_gnn_be1': _L3_gnn_in['be1'], 'L3_gnn_We2': _L3_gnn_in['We2'], 'L3_gnn_be2': _L3_gnn_in['be2'], 'L3_gnn_Wu1': _L3_gnn_in['Wu1'], 'L3_gnn_bu1': _L3_gnn_in['bu1'], 'L3_gnn_Wu2': _L3_gnn_in['Wu2'], 'L3_gnn_bu2': _L3_gnn_in['bu2'], 'L3_gnn_gamma': _L3_gnn_in['gamma'], 'L3_gnn_beta': _L3_gnn_in['beta']}

def reference(x, src, dst, edge_weight, L0_gnn_W1, L0_gnn_b1, L0_gnn_W2, L0_gnn_b2, L1_gnn_W, L1_gnn_b, L2_gnn_W_self1, L2_gnn_W_neigh1, L2_gnn_b1, L2_gnn_W_self2, L2_gnn_W_neigh2, L2_gnn_b2, L3_gnn_We1, L3_gnn_be1, L3_gnn_We2, L3_gnn_be2, L3_gnn_Wu1, L3_gnn_bu1, L3_gnn_Wu2, L3_gnn_bu2, L3_gnn_gamma, L3_gnn_beta):
    import jax
    import jax.numpy as jnp

    def _L0_gnn_ref(features, src, dst, W1, b1, W2, b2):
        import jax, jax.numpy as jnp
        import numpy as np
        N_NODES = 3125
        N_EDGES = 50000
        IN_FEATS = 128
        H_FEATS = 128

        def _degree_norms(src, dst, n_nodes):
            ones = jnp.ones(src.shape[0], dtype=jnp.float32)
            deg_out = jax.ops.segment_sum(ones, src, num_segments=n_nodes)
            deg_in = jax.ops.segment_sum(ones, dst, num_segments=n_nodes)
            norm_src = jax.lax.rsqrt(jnp.maximum(deg_out, 1.0))
            norm_dst = jax.lax.rsqrt(jnp.maximum(deg_in, 1.0))
            return (norm_src, norm_dst)

        def _graph_conv(x, W, b, src, dst, norm_src, norm_dst, n_nodes):
            h = x * norm_src[:, None] @ W
            msgs = jnp.take(h, src, axis=0)
            agg = jax.ops.segment_sum(msgs, dst, num_segments=n_nodes)
            return agg * norm_dst[:, None] + b
        n_nodes = features.shape[0]
        norm_src, norm_dst = _degree_norms(src, dst, n_nodes)
        h = _graph_conv(features, W1, b1, src, dst, norm_src, norm_dst, n_nodes)
        h = jax.nn.relu(h)
        h = _graph_conv(h, W2, b2, src, dst, norm_src, norm_dst, n_nodes)
        return h

    def _L1_gnn_ref(x, W, b, src, dst):
        import jax, jax.numpy as jnp
        import numpy as np
        N_NODES = 50000
        N_EDGES = 25000
        IN_FEATS = 128
        N_CLASSES = 128
        n = x.shape[0]
        msg_sum = jax.ops.segment_sum(x[src], dst, num_segments=n)
        deg = jax.ops.segment_sum(jnp.ones_like(dst, dtype=x.dtype), dst, num_segments=n)
        neigh_mean = msg_sum / jnp.maximum(deg, 1.0)[:, None]
        h = jnp.concatenate([x, neigh_mean], axis=1)
        return h @ W.T + b

    def _L2_gnn_ref(x, src, dst, W_self1, W_neigh1, b1, W_self2, W_neigh2, b2):
        import jax, jax.numpy as jnp
        import numpy as np
        N_NODES = 50000
        N_EDGES = 25000
        IN_FEATS, HID_FEATS, OUT_FEATS = (128, 256, 128)
        N = x.shape[0]
        deg = jax.ops.segment_sum(jnp.ones((src.shape[0],), dtype=x.dtype), dst, num_segments=N)
        deg = jnp.maximum(deg, 1.0)[:, None]

        def sage_conv(h, W_self, W_neigh, b):
            agg = jax.ops.segment_sum(h[src], dst, num_segments=N) / deg
            return h @ W_self + agg @ W_neigh + b
        h = jax.nn.relu(sage_conv(x, W_self1, W_neigh1, b1))
        return sage_conv(h, W_self2, W_neigh2, b2)

    def _L3_gnn_ref(hidden, edge_index, edge_weight, We1, be1, We2, be2, Wu1, bu1, Wu2, bu2, gamma, beta):
        import jax, jax.numpy as jnp
        import numpy as np
        HID = 128
        N_NODES = 50000
        N_EDGES = 18750

        def _layernorm(x, gamma, beta, eps=1e-05):
            mu = jnp.mean(x, axis=-1, keepdims=True)
            var = jnp.var(x, axis=-1, keepdims=True)
            return (x - mu) * jax.lax.rsqrt(var + eps) * gamma + beta
        src, dst = (edge_index[0], edge_index[1])
        edge_inputs = jnp.concatenate([hidden[src], hidden[dst], edge_weight[:, None]], axis=1)
        h = jax.nn.gelu(edge_inputs @ We1 + be1, approximate=False)
        messages = h @ We2 + be2
        aggregated = jax.ops.segment_sum(messages, dst, num_segments=hidden.shape[0])
        u = jnp.concatenate([hidden, aggregated], axis=1)
        u = jax.nn.gelu(u @ Wu1 + bu1, approximate=False)
        updated = u @ Wu2 + bu2
        return _layernorm(hidden + updated, gamma, beta)
    edge_index = jnp.stack([src, dst])
    h = jnp.maximum(_layernorm(x, axis=-1), 0.0)
    x = x + _L0_gnn_ref(h, src, dst, L0_gnn_W1, L0_gnn_b1, L0_gnn_W2, L0_gnn_b2)
    h = jnp.maximum(_layernorm(x, axis=-1), 0.0)
    x = x + _L1_gnn_ref(h, L1_gnn_W, L1_gnn_b, src, dst)
    h = jnp.maximum(_layernorm(x, axis=-1), 0.0)
    x = x + _L2_gnn_ref(h, src, dst, L2_gnn_W_self1, L2_gnn_W_neigh1, L2_gnn_b1, L2_gnn_W_self2, L2_gnn_W_neigh2, L2_gnn_b2)
    h = jnp.maximum(_layernorm(x, axis=-1), 0.0)
    x = x + _L3_gnn_ref(h, edge_index, edge_weight, L3_gnn_We1, L3_gnn_be1, L3_gnn_We2, L3_gnn_be2, L3_gnn_Wu1, L3_gnn_bu1, L3_gnn_Wu2, L3_gnn_bu2, L3_gnn_gamma, L3_gnn_beta)
    return x

_drawn_inputs = setup_inputs


def setup_inputs(seed=0):
    import zlib

    import numpy as np

    out = dict(_drawn_inputs(seed))
    spreads = {'L0_gnn_b1': (0.0, 0.1),
     'L0_gnn_b2': (0.0, 0.1),
     'L2_gnn_b1': (0.0, 0.1),
     'L2_gnn_b2': (0.0, 0.1),
     'L3_gnn_be1': (0.0, 0.8),
     'L3_gnn_be2': (0.0, 0.42),
     'L3_gnn_bu1': (0.0, 0.31),
     'L3_gnn_bu2': (0.0, 0.1),
     'L3_gnn_gamma': (1.0, 0.2),
     'L3_gnn_beta': (0.0, 0.1)}
    factors = {'edge_weight': 8.0, 'L3_gnn_We1': 3.233, 'L3_gnn_We2': 2.852}
    for name, (base, spread) in spreads.items():
        noise = np.random.default_rng([zlib.crc32(name.encode()), seed]).standard_normal(out[name].shape)
        drawn = base * np.exp(spread * noise) if base else spread * noise
        out[name] = jnp.asarray(drawn.astype(out[name].dtype))
    for name, factor in factors.items():
        out[name] = (out[name] * factor).astype(out[name].dtype)
    return out
```

```python
from contextlib import ExitStack

import concourse.bass as bass
from concourse import mybir

F32 = mybir.dt.float32
F16 = mybir.dt.float16
I32 = mybir.dt.int32
ALU = mybir.AluOpType
ACT = mybir.ActivationFunctionType
ds = bass.ds

P = 128
NODES = 50000
EDGES = 50000
BLOCKS = 392
TILES = 392
NP = BLOCKS * P
PAD_NODE = NP - 1
STEPS = TILES + BLOCKS - 1
US = 27
SPINS = STEPS // US
SUMS = 9
LAPS = STEPS // SUMS
RING = 14
CH = 7
CHUNKS = TILES // CH
NLOADS = 23
TABW = [512, STEPS + 2 - 512, 512, STEPS + 2 - 512, TILES]
LEAD = 2
WS = STEPS + LEAD
Q4 = 4
BC = BLOCKS // Q4
GROUPS = BLOCKS // Q4
TURNS = GROUPS // 2
EPS = 1e-5
CREDIT = 9
assert SPINS * US == STEPS and NP >= NODES and CHUNKS % 2 == 0


class Chain:

    def __init__(self, eng, sem):
        self.eng, self.sem, self.done, self.i, self.k, self.per = eng, sem, 0, None, 0, 0

    def turn(self, i, per):
        self.i, self.k, self.per = i, 0, per

    def over(self, n):
        assert self.k == self.per, (self.k, self.per)
        self.done += n * self.per
        self.i = None

    def link(self, ins):
        ins.then_inc(self.sem, 1)
        if self.i is None:
            self.done += 1
            self.eng.wait_ge(self.sem, self.done)
        else:
            self.k += 1
            self.eng.wait_ge(self.sem, self.i * self.per + (self.done + self.k))


def program(nc, a, out):
    with ExitStack() as ctx:
        def sb(name, shape, dt=F32):
            return ctx.enter_context(nc.sbuf_tensor(name, shape, dt))

        def sem(name):
            return ctx.enter_context(nc.semaphore(name))

        def pair(name):
            return [sem(f"{name}{k}") for k in range(2)]

        def dram(name, shape, dt=F32):
            return nc.dram_tensor(name, shape, dt).ap()

        edges = dram("edges_by_block", [NP, 4], I32)
        x_pad = dram("x_pad", [NP, P])
        agg = dram("agg", [BLOCKS + STEPS, P, P])
        tabs = [dram("table_a", [NP, P]), dram("table_b", [NP, P])]
        q_tab = dram("table_dst", [NP, P])
        h5_d = dram("h5_rows", [NP, P])
        state = dram("state", [NP, P])
        rdeg_row = dram("rdeg_row", [BLOCKS, P])
        deg_row = dram("deg_row", [BLOCKS, P])

        def rows(t, g):
            return t.rearrange("(g j p) d -> g p j d", j=Q4, p=P)[g]

        def sums(g):
            return agg.rearrange("b f n -> f b n")[:, ds(g * Q4, Q4), :]

        ident = sb("ident", [P, P]); ones = sb("ones", [P, P]); zero = sb("zero", [P, P])
        iota_i = sb("iota_i", [P, WS], I32); iota_f = sb("iota_f", [P, WS])
        iota_h = sb("iota_h", [P, BLOCKS], F16)
        upper = sb("upper", [P, P]); upper_h = sb("upper_h", [P, P], F16)
        lower_h = sb("lower_h", [P, P], F16); ones_h = sb("ones_h", [P, P], F16)
        zero_h = sb("zero_h", [P, P], F16)
        part_i = sb("part_i", [P, 1], I32); part_f = sb("part_f", [P, 1])
        src_o = sb("src_o", [P, TILES], I32); dst_o = sb("dst_o", [P, TILES], I32)
        ew_o = sb("ew_o", [P, TILES])
        cut_i = sb("cut_i", [P, TILES], I32)
        slo = sb("slo", [P, TILES]); shi = sb("shi", [P, TILES])
        dlo = sb("dlo", [P, TILES]); dhi = sb("dhi", [P, TILES + 1])
        oh_lo = sb("oh_lo", [P, 4, P], F16); oh_hi = sb("oh_hi", [P, 4, BLOCKS], F16)
        oh_bk = sb("oh_bk", [P, CH, BLOCKS], F16)
        junk = sb("junk", [P, 2, BLOCKS])
        deg = sb("deg", [P, BLOCKS]); nsrc = sb("nsrc", [P, BLOCKS])
        ndst = sb("ndst", [P, BLOCKS]); rdeg = sb("rdeg", [P, BLOCKS])
        cnt = sb("cnt", [BC, Q4]); cum = sb("cum", [BC, Q4]); before = sb("before", [BC, Q4])
        before_i = sb("before_i", [BC, Q4], I32); first = sb("first", [BC, Q4])
        start = sb("start", [BC, Q4]); diag = sb("diag", [BC, Q4, BC]); blk = sb("blk", [BC, Q4])
        ge = sb("ge", [BC, 512])
        b_row = sb("b_row", [P, WS]); keep = sb("keep", [P, WS]); t_row = sb("t_row", [1, WS])
        dest_f = sb("dest_f", [1, WS]); ls_row = sb("ls_row", [1, TILES])
        tab_t = sb("tab_t", [1, WS], I32); tab_dest = sb("tab_dest", [1, WS], I32)
        tab_last = sb("tab_last", [1, TILES], I32)
        posf = sb("posf", [P, 2 * CH])
        pos_i = [sb(f"pos_i{k}", [P, CH], I32) for k in range(2)]
        pack = [sb(f"pack{k}", [P, CH, 4], I32) for k in range(2)]
        e_in = sb("e_in", [BC, Q4, P * 4], I32); e_f = sb("e_f", [BC, P])
        srcT = sb("srcT", [P, TILES], I32); dstT = sb("dstT", [P, TILES], I32)
        dstF = sb("dstF", [P, TILES]); ewT = sb("ewT", [P, TILES])
        dstrel = sb("dstrel", [P, WS])
        six = [sb(f"six{k}", [P, CH], I32) for k in range(2)]
        dix = [sb(f"dix{k}", [P, CH], I32) for k in range(2)]
        M = sb("M", [P, RING, P]); GE = sb("GE", [P, RING, P])
        OH = sb("OH", [P, 3, P]); ACC = sb("ACC", [P, SUMS, P])
        w1 = sb("w1", [P, P]); w2 = sb("w2", [P, P])
        wl = sb("wl", [P, 2 * P]); wlT = sb("wlT", [P, 2, P])
        ws1 = sb("ws1", [P, 2 * P]); wn1 = sb("wn1", [P, 2 * P])
        w42 = sb("w42", [P, 2, 2, P])
        we1 = sb("we1", [P, 2, P]); we2 = sb("we2", [P, P])
        wu1 = sb("wu1", [P, 2, P]); wu2 = sb("wu2", [P, P])
        bias = sb("bias", [1, 8, P])
        b1col = sb("b1col", [P, 2]); bu1col = sb("bu1col", [P, 1])
        b1bc = sb("b1bc", [P, P]); b2bc = sb("b2bc", [P, P]); we1c = sb("we1c", [P, P])
        gam = sb("gam", [P, P]); bet = sb("bet", [P, P])
        gam4 = sb("gam4", [P, 512]); bet4 = sb("bet4", [P, 512]); b2x4 = sb("b2x4", [P, 512])
        bz = sb("bz", [1, 3, 2 * P])
        bz4 = bz[:, 0, :]; bz5 = bz[:, 1, :]
        IN = sb("IN", [P, 2, 512]); XB = sb("XB", [P, 2, 512]); HB = sb("HB", [P, 2, 512])
        HT = sb("HT", [P, 2, 512]); Z = sb("Z", [P, 2, 512]); HO = sb("HO", [P, 2, 512])
        T1 = sb("T1", [P, 2, 512]); T2 = sb("T2", [P, 2, 512]); RB = sb("RB", [P, 2, 512])
        OB = sb("OB", [P, 2, 512]); AG = sb("AG", [P, 2, 512])
        MV = sb("MV", [P, 2, Q4, 2]); ST = sb("ST", [P, 2, Q4, 6])
        SC = sb("SC", [P, 2, Q4]); BI = sb("BI", [P, 2, Q4]); VE = sb("VE", [P, 2, Q4]); NM = sb("NM", [P, 2, Q4])
        mhalf = sb("mhalf", [P, BLOCKS])

        ps = [ctx.enter_context(nc.psum_tensor(f"ps{k}", [P, 512], F32)) for k in range(8)]

        def q(t):
            return t.rearrange("p (j d) -> p j d", j=Q4)

        s_const = sem("consts_made"); s_cv = sem("consts_cast"); s_load = sem("edges_loaded")
        s_pad = sem("padding_set"); s_w = sem("weights_loaded"); s_xp = sem("x_padded")
        s_w42 = sem("w_transposed"); s_split = sem("ids_split")
        s_oh = sem("hist_onehots"); s_hist = sem("hist_columns"); s_hz = sem("hist_cleared")
        s_deg = sem("degrees_read"); s_cnt = sem("block_counts"); s_cntc = sem("block_counts_read")
        s_cum = sem("before_counts"); s_deg1 = sem("degrees_clamped"); s_pow = sem("norms_made"); s_tabm = sem("table_products"); s_tabr = sem("table_reads")
        s_ge = sem("table_masks")
        s_diag = sem("diag_made"); s_base = sem("rank_bases"); s_rk = sem("rank_onehots")
        s_rank = sem("rank_products"); s_rr = sem("rank_reads"); s_pack = pair("rows_packed")
        s_scat = pair("rows_placed"); s_el = sem("sorted_loaded"); s_ec = sem("sorted_cast")
        s_et = sem("sorted_turned"); s_er = sem("sorted_read"); s_rel = sem("walk_ready")
        s_dt = sem("deg_turned"); s_dc = sem("deg_copied"); s_dr = sem("deg_rows_stored")
        s_wt = sem("lin_turned")
        pe_steps = sem("pe_steps"); acc_steps = sem("acc_steps"); oh_done = sem("onehots_done")
        tiles_ready = sem("tiles_ready"); idx_ready = sem("idx_ready")
        gathered = [sem(f"gathered{k}") for k in range(RING)]
        out_done = [sem(f"sum_written{k}") for k in range(SUMS)]
        slots_set = sem("slots_set"); gelu_own = sem("gelu_done")
        paced = sem("paced")
        link_v = sem("vector_link"); link_p = sem("pool_link")
        D = {w: pair(f"dense_{w}_") for w in "in stat coef out st mm z tr ht mean mma hid ev at mmb mmc gl nrm".split()}
        IN_, STAT, COEF, OUT, ST_, MM, Z_, TR, HT_ = (D[w] for w in "in stat coef out st mm z tr ht".split())
        MEAN, MMA, HID, EV, AT, MMB, MMC, GL, NRM = (D[w] for w in "mean mma hid ev at mmb mmc gl nrm".split())
        USES = {"in": [16, 16, 32, 32, 64, 32, 64], "st": [16, 16, 32, 32, 32, 64, 16],
                "coef": [1, 0, 0, 0, 0, 0, 0], "stat": [1, 0, 1, 1, 0, 1, 1], "out": [1] * 7, "mm": [1, 1, 1, 0, 1, 1, 0],
                "z": [0, 1, 1, 1, 1, 1, 1], "tr": [1, 1, 1, 0, 1, 1, 1], "ht": [1, 1, 1, 0, 1, 1, 1],
                "ev": [0, 0, 1, 0, 0, 1, 0], "gl": [1, 1, 1, 0, 0, 0, 1], "mma": [0, 0, 0, 0, 1, 0, 1]}

        def at(d, w):
            return TURNS * sum(USES[w][:d]) if w in USES else 0

        block = ctx.enter_context(nc.Block())

        def from_table(eng, table, at_, n, most):
            return nc.values_load_multi_w_load_instructions(table[0:1, ds(at_, n)], engines=[eng.engine],
                                                            min_val=0, max_val=most)[1]

        def stand(eng):
            eng.sem_inc(paced, 1)

        def written(eng, ph):
            for k in range(SUMS):
                eng.wait_ge(out_done[k], 16 * LAPS * (ph + 1))

        def stored(eng, d):
            for k in range(2):
                eng.wait_ge(ST_[k], at(d + 1, "st"))

        @block.sync
        def _(sp):
            full = NP // P
            whole = EDGES // full
            sp.wait_ge(s_pad, 3)
            for t, name in ((src_o, "src"), (dst_o, "dst"), (ew_o, "edge_weight")):
                sp.dma_start(t[0:whole, :], a[name][0:whole * full].rearrange("(p c) -> p c", c=full)).then_inc(s_load, 16)
                sp.dma_start(t[whole:whole + 1, 0:EDGES - whole * full],
                             a[name][whole * full:EDGES].rearrange("(p c) -> p c", p=1)).then_inc(s_load, 16)
            sp.wait_ge(s_const, 3)
            sp.dma_start(x_pad[0:NODES].rearrange("(s b) d -> s (b d)", s=16),
                         a["x"].rearrange("(s b) d -> s (b d)", s=16)).then_inc(s_xp, 16)
            sp.dma_start(x_pad[NODES:NODES + P], zero[:, :]).then_inc(s_xp, 16)
            sp.dma_start(x_pad[NODES + P:NP], zero[0:NP - NODES - P, :]).then_inc(s_xp, 16)
            r1 = lambda v: v.rearrange("(o n) -> o n", o=1)
            bc = lambda v: v.rearrange("(o n) -> o n", o=1).broadcast_to([P, P])
            loads = [
                (w1[:, :], a["L0_gnn_W1"]), (w2[:, :], a["L0_gnn_W2"]), (wl[:, :], a["L1_gnn_W"]),
                (ws1[:, :], a["L2_gnn_W_self1"]), (wn1[:, :], a["L2_gnn_W_neigh1"]),
                (w42[:, :, 0, :], a["L2_gnn_W_neigh2"].rearrange("(h p) n -> p h n", h=2)),
                (w42[:, :, 1, :], a["L2_gnn_W_self2"].rearrange("(h p) n -> p h n", h=2)),
                (we1[:, :, :], a["L3_gnn_We1"][0:2 * P].rearrange("(h p) n -> p h n", h=2)),
                (we2[:, :], a["L3_gnn_We2"]),
                (wu1[:, :, :], a["L3_gnn_Wu1"].rearrange("(h p) n -> p h n", h=2)),
                (wu2[:, :], a["L3_gnn_Wu2"]),
                (bias[:, 2, :], r1(a["L1_gnn_b"])), (bias[:, 3, :], r1(a["L2_gnn_b2"])),
                (bias[:, 4, :], r1(a["L3_gnn_be1"])), (bias[:, 5, :], r1(a["L3_gnn_be2"])),
                (bias[:, 6, :], r1(a["L3_gnn_bu2"])),
                (b1col[:, :], a["L2_gnn_b1"].rearrange("(h p) -> p h", h=2)),
                (bu1col[:, :], a["L3_gnn_bu1"].rearrange("(p o) -> p o", o=1)),
                (b1bc[:, :], bc(a["L0_gnn_b1"])), (b2bc[:, :], bc(a["L0_gnn_b2"])),
                (we1c[:, :], a["L3_gnn_We1"][2 * P:2 * P + 1].broadcast_to([P, P])),
                (gam[:, :], bc(a["L3_gnn_gamma"])), (bet[:, :], bc(a["L3_gnn_beta"])),
            ]
            assert len(loads) == NLOADS
            for dst_, src_ in loads:
                sp.dma_start(dst_, src_, allow_slow_non_contiguous=True).then_inc(s_w, 16)

            sp.wait_ge(s_xp, 48)
            with sp.Fori(0, TURNS) as i:
                for b in range(2):
                    sp.wait_ge(OUT[b], i + at(0, "out"))
                    sp.dma_start(q(XB[:, b, :]), rows(x_pad, 2 * i + b)).then_inc(IN_[b], 16)
            for k in range(2):
                sp.wait_ge(s_scat[k], 16 * TILES // 2)
            for k in range(Q4):
                sp.dma_start(e_in[:, k, :], edges.rearrange("(k t p) f -> k t (p f)", k=Q4, p=P)[k]).then_inc(s_el, 16)
            sp.wait_ge(s_dc, 1)
            for k, t in enumerate((rdeg_row, deg_row)):
                sp.dma_start(t.rearrange("(k c) p -> c k p", k=Q4), q(OB[0:BC, k, :])).then_inc(s_dr, 16)

            sp.wait_ge(s_dr, 32)

            def walk(ph):
                sp.wait_ge(s_rel, 1)
                with sp.Fori(0, SPINS) as i:
                    places = from_table(sp, tab_dest, i * US, US, BLOCKS + STEPS - 1)
                    for j, to in enumerate(places):
                        s = i * US + j
                        sp.wait_ge(acc_steps, s + (CREDIT + STEPS * ph + 1))
                        sp.dma_start(agg.rearrange("b f n -> f b n")[:, ds(to, 1), :].rearrange("f o n -> f (o n)"), ACC[:, j % SUMS, :]).then_inc(out_done[j % SUMS], 16)
                written(sp, ph)

            walk(0)
            with sp.Fori(0, TURNS) as i:
                for b in range(2):
                    sp.wait_ge(Z_[b], i + at(1, "z"))
                    sp.dma_start(q(IN[:, b, :]), sums(i * 2 + b)).then_inc(IN_[b], 16)
            for d, base in ((2, x_pad), (3, state)):
                walk(d - 1)
                with sp.Fori(0, TURNS) as i:
                    for b in range(2):
                        sp.wait_ge(Z_[b], i + at(d, "z"))
                        sp.dma_start(q(IN[:, b, :]), sums(i * 2 + b)).then_inc(IN_[b], 16)
                        sp.dma_start(q(XB[:, b, :]), rows(base, i * 2 + b)).then_inc(IN_[b], 16)
            walk(3)
            sp.wait_ge(s_dr, 32)
            with sp.Fori(0, TURNS) as i:
                for b in range(2):
                    g = 2 * i + b
                    sp.wait_ge(MM[b], i + at(4, "mm"))
                    sp.dma_start(q(IN[:, b, :]), sums(g)).then_inc(IN_[b], 16)
                    sp.dma_start(RB[:, b, :], rdeg_row.rearrange("(g j) p -> g (j p)", j=Q4)[ds(g, 1), :].broadcast_to([P, 512])).then_inc(IN_[b], 16)
                    sp.dma_start(q(HB[:, b, :]), rows(tabs[1], g)).then_inc(IN_[b], 16)
                    sp.wait_ge(Z_[b], i + at(4, "z"))
                    sp.dma_start(q(XB[:, b, :]), rows(state, g)).then_inc(IN_[b], 16)
            stored(sp, 4)
            walk(4)
            with sp.Fori(0, TURNS) as i:
                for b in range(2):
                    sp.wait_ge(Z_[b], i + at(5, "z"))
                    sp.dma_start(q(IN[:, b, :]), sums(2 * i + b)).then_inc(IN_[b], 16)
                    sp.dma_start(q(XB[:, b, :]), rows(state, 2 * i + b)).then_inc(IN_[b], 16)
            stored(sp, 5)
            walk(5)
            with sp.Fori(0, TURNS) as i:
                for b in range(2):
                    g = 2 * i + b
                    sp.wait_ge(MMB[b], i + at(6, "mmb"))
                    sp.dma_start(q(IN[:, b, :]), sums(g)).then_inc(IN_[b], 16)
                    sp.dma_start(RB[0:1, b, :], deg_row.rearrange("(g j) p -> g (j p)", j=Q4)[ds(g, 1), :]).then_inc(IN_[b], 16)
                    sp.wait_ge(OUT[b], i + at(6, "out"))
                    sp.dma_start(q(HB[:, b, :]), rows(h5_d, g)).then_inc(IN_[b], 16)
                    sp.dma_start(q(XB[:, b, :]), rows(state, g)).then_inc(IN_[b], 16)

        @block.gpsimd
        def _(pool):
            nc.gpsimd.memset(src_o[:], PAD_NODE).then_inc(s_pad, 1)
            nc.gpsimd.memset(dst_o[:], PAD_NODE).then_inc(s_pad, 1)
            nc.gpsimd.memset(ew_o[:], 0.0).then_inc(s_pad, 1)
            nc.gpsimd.memset(mhalf[:], -0.5)
            nc.gpsimd.memset(ones[:], 1.0).then_inc(s_const, 1)
            nc.gpsimd.memset(zero[:], 0.0).then_inc(s_const, 1)
            nc.gpsimd.iota(iota_i[:], [[1, WS]], base=0, channel_multiplier=0).then_inc(s_const, 1)
            nc.gpsimd.iota(part_i[:], [[1, 1]], base=0, channel_multiplier=1).then_inc(s_const, 1)
            pool.wait_ge(s_const, 4)
            nc.gpsimd.affine_select(out=ident[:], in_=zero[:], compare_op=ALU.not_equal, fill=1.0, base=0,
                                    pattern=[[-1, P]], channel_multiplier=1).then_inc(s_const, 1)
            nc.gpsimd.affine_select(out=upper[:], in_=zero[:], compare_op=ALU.is_ge, fill=1.0, base=0,
                                    pattern=[[-1, P]], channel_multiplier=1).then_inc(s_const, 1)
            pool.wait_ge(s_deg1, 1)
            for t in (nsrc, ndst):
                nc.gpsimd.tensor_tensor(t[:, :], t[:, :], mhalf[:, :], ALU.pow).then_inc(s_pow, 1)

            with pool.Fori(0, CHUNKS // 2) as i:
                for b in range(2):
                    pool.wait_ge(s_pack[b], i + 1)
                    stand(pool)
                    for j in range(CH):
                        nc.gpsimd.indirect_dma_start(
                            out=edges, out_offset=bass.IndirectOffsetOnAxis(ap=pos_i[b][:, j:j + 1], axis=0),
                            in_=pack[b][:, j, :], in_offset=None).then_inc(s_scat[b], 16)

            chain = Chain(pool, link_p)
            link = chain.link

            def coefficients(d, scaled=False):
                with pool.Fori(0, TURNS) as i:
                    chain.turn(i, 2 * (3 + scaled))
                    for b in range(2):
                        pool.wait_ge(STAT[b], i + (at(d, "stat") + 1))
                        stand(pool)
                        nc.gpsimd.tensor_scalar(NM[:, b, :], MV[:, b, :, 0], -1.0, None, ALU.mult)
                        link(nc.gpsimd.tensor_scalar(VE[:, b, :], MV[:, b, :, 1], EPS, None, ALU.add))
                        link(nc.gpsimd.tensor_tensor(SC[:, b, :], VE[:, b, :], mhalf[:, 0:Q4], ALU.pow))
                        if scaled:
                            link(nc.gpsimd.tensor_tensor(SC[:, b, :], SC[:, b, :], nsrc[:, ds(i * 2 * Q4 + b * Q4, Q4)], ALU.mult))
                        link(nc.gpsimd.tensor_tensor(BI[:, b, :], NM[:, b, :], SC[:, b, :], ALU.mult))
                        pool.sem_inc((COEF if d == 0 else Z_)[b], 1)
                    chain.over(TURNS)

            pool.wait_ge(s_pow, 2)
            coefficients(0, True)

            def gather(table, idx, slot, done, add):
                nc.gpsimd.indirect_dma_start(
                    out=M[:, slot, :], out_offset=None, in_=table,
                    in_offset=bass.IndirectOffsetOnAxis(ap=idx, axis=0),
                    **({"compute_op": ALU.add} if add else {})).then_inc(done, 16)

            def walk(ph, table, d):
                stored(pool, d)

                def chunk(b, ready, last):
                    pool.wait_ge(idx_ready, ready)
                    if last is not None:
                        pool.wait_ge(pe_steps, last)
                    stand(pool)
                    for j in range(CH):
                        gather(table, six[b][:, j:j + 1], b * CH + j, gathered[b * CH + j], False)

                for b in range(2):
                    chunk(b, CHUNKS * ph + b + 1, None)
                with pool.Fori(1, CHUNKS // 2) as i:
                    for b in range(2):
                        last = pool.value_load(tab_last[0:1, ds(i * 2 * CH + ((b - 1) * CH - 1), 1)], min_val=0, max_val=STEPS - 1)
                        chunk(b, i * 2 + (CHUNKS * ph + b + 1), last + (CREDIT + STEPS * ph + 1))

            walk(0, tabs[0], 0)
            walk(1, tabs[1], 1)
            coefficients(2)
            walk(2, tabs[0], 2)
            coefficients(3)
            walk(3, tabs[1], 3)
            walk(4, tabs[0], 4)
            coefficients(5)
            stored(pool, 5)
            with pool.Fori(0, CHUNKS // 2) as i:
                for b in range(2):
                    pool.wait_ge(slots_set, i * 2 + (b + 1))
                    stand(pool)
                    for j in range(CH):
                        gather(tabs[1], six[b][:, j:j + 1], b * CH + j, gathered[b * CH + j], True)
                    for j in range(CH):
                        pool.wait_ge(gathered[b * CH + j], i * 32 + 16 * (5 * (CHUNKS // 2) + 1))
                        stand(pool)
                        gather(q_tab, dix[b][:, j:j + 1], b * CH + j, gathered[b * CH + j], True)

            coefficients(6)

        @block.scalar
        def _(act):
            def relu(dst_, src_, scale, bias_=0.0, func=ACT.Relu):
                return nc.scalar.activation(dst_, src_, func, bias=bias_, scale=scale)

            def normed(d, i, b, src_, dst_, coef, out_):
                act.wait_ge(D[coef][b], i + 1 + at(d, coef))
                if d == 3:
                    act.wait_ge(ST_[b], i * 32 + at(3, "st"))
                elif d == 5:
                    act.wait_ge(ST_[b], i * 64 + at(5, "st"))
                    act.wait_ge(TR[b], i + at(5, "tr"))
                else:
                    act.wait_ge(TR[b], i + at(d, "tr"))
                stand(act)
                for j in range(Q4):
                    last = relu(dst_[:, j, :], src_[:, j, :], SC[:, b, j:j + 1], BI[:, b, j:j + 1])
                last.then_inc(D[out_][b], 1)
                act.wait_ge(D[out_][b], i + 1 + at(d, out_))

            def store(d, b, t, buf, g):
                act.dma_start(rows(t, g), q(buf[:, b, :])).then_inc(ST_[b], 16)

            def to_table(d, i, b):
                act.wait_ge(TR[b], i + (at(d, "tr") + 1))
                act.wait_ge(MM[b], i + at(d, "mm"))
                stand(act)
                nc.scalar.activation(HT[:, b, :], ps[b][:, :], ACT.Copy).then_inc(HT_[b], 1)
                act.wait_ge(MM[b], i + (at(d, "mm") + 1))
                act.wait_ge(ST_[b], i * USES["st"][d] + at(d, "st"))
                stand(act)
                product = ps[2 + b] if d < 2 else ps[2 + 2 * b]
                nc.scalar.activation(T1[:, b, :], product[:, :], ACT.Copy).then_inc(GL[b], 1)
                act.wait_ge(GL[b], i + (at(d, "gl") + 1))
                store(d, b, tabs[d % 2], T1, i * 2 + b)

            with act.Fori(0, TURNS) as i:
                for b in range(2):
                    normed(0, i, b, q(XB[:, b, :]), q(HO[:, b, :]), "coef", "out")
                    to_table(0, i, b)

            def lists(h, b, ready):
                nc.scalar.activation(six[b][:, :], srcT[:, ds(h * CH, CH)], ACT.Copy).then_inc(ready, 1)

            def walk(ph):
                def forward(b, value):
                    for j in range(CH):
                        act.wait_ge(gathered[b * CH + j], value)
                        act.sem_inc(tiles_ready, 1)

                lists(0, 0, idx_ready)
                with act.Fori(0, CHUNKS // 2 - 1) as i:
                    for b in range(2):
                        lists(i * 2 + (b + 1), 1 - b, idx_ready)
                        forward(b, i * 16 + 16 * (CHUNKS // 2 * ph + 1))
                h = CHUNKS - 2
                lists(h + 1, 1, idx_ready)
                for b in range(2):
                    forward(b, 16 * CHUNKS // 2 * (ph + 1))

            act.wait_ge(s_rel, 1)
            act.wait_ge(s_pow, 2)
            walk(0)
            with act.Fori(0, TURNS) as i:
                for b in range(2):
                    act.wait_ge(Z_[b], i + (at(1, "z") + 1))
                    act.wait_ge(TR[b], i + at(1, "tr"))
                    stand(act)
                    for j in range(Q4):
                        last = relu(q(HO[:, b, :])[:, j, :], q(Z[:, b, :])[:, j, :], nsrc[:, ds(i * 2 * Q4 + (b * Q4 + j), 1)])
                    last.then_inc(OUT[b], 1)
                    to_table(1, i, b)
            walk(1)
            with act.Fori(0, TURNS) as i:
                for b in range(2):
                    normed(2, i, b, q(Z[:, b, :]), q(HO[:, b, :]), "z", "out")
                    to_table(2, i, b)
                    act.wait_ge(EV[b], i + (at(2, "ev") + 1))
                    store(2, b, state, T2, i * 2 + b)
            walk(2)
            with act.Fori(0, TURNS) as i:
                for b in range(2):
                    normed(3, i, b, q(Z[:, b, :]), q(HO[:, b, :]), "z", "out")
                    store(3, b, tabs[1], HO, i * 2 + b)
                    store(3, b, state, Z, i * 2 + b)
            walk(3)
            with act.Fori(0, TURNS) as i:
                for b in range(2):
                    act.wait_ge(TR[b], i + 1 + at(4, "tr"))
                    act.wait_ge(MMA[b], i + at(4, "mma"))
                    stand(act)
                    nc.scalar.activation(HT[:, b, :], ps[b][:, :], ACT.Copy).then_inc(HT_[b], 1)
                    act.wait_ge(MMA[b], i + 1 + at(4, "mma"))
                    act.wait_ge(MM[b], i + at(4, "mm"))
                    stand(act)
                    nc.scalar.activation(T1[:, b, :], ps[2][:, :], ACT.Relu, bias=b1col[:, 0:1])
                    nc.scalar.activation(T2[:, b, :], ps[3][:, :], ACT.Relu, bias=b1col[:, 1:2]).then_inc(HID[b], 1)
                    act.wait_ge(MM[b], i + 1 + at(4, "mm"))
                    act.wait_ge(ST_[b], i * 32 + at(4, "st"))
                    stand(act)
                    nc.scalar.activation(HO[:, b, :], ps[4][:, :], ACT.Copy).then_inc(OUT[b], 1)
                    act.wait_ge(OUT[b], i + 1 + at(4, "out"))
                    store(4, b, tabs[0], HO, 2 * i + b)
                    act.wait_ge(Z_[b], i + 1 + at(4, "z"))
                    store(4, b, state, Z, 2 * i + b)
            walk(4)
            with act.Fori(0, TURNS) as i:
                for b in range(2):
                    g = 2 * i + b
                    normed(5, i, b, q(Z[:, b, :]), q(HO[:, b, :]), "z", "out")
                    store(5, b, h5_d, HO, g)
                    store(5, b, state, Z, g)
                    act.wait_ge(TR[b], i + 1 + at(5, "tr"))
                    act.wait_ge(MM[b], i + at(5, "mm"))
                    stand(act)
                    nc.scalar.activation(HT[:, b, :], ps[b][:, :], ACT.Copy).then_inc(HT_[b], 1)
                    act.wait_ge(EV[b], i + 1 + at(5, "ev"))
                    store(5, b, tabs[1], T1, g)
                    store(5, b, q_tab, T2, g)
            stored(act, 5)
            half = CHUNKS // 2

            def prepare(h, b):
                nc.scalar.activation(six[b][:, :], srcT[:, ds(h * CH, CH)], ACT.Copy)
                nc.scalar.activation(dix[b][:, :], dstT[:, ds(h * CH, CH)], ACT.Copy)
                for j in range(CH):
                    last = nc.scalar.activation(M[:, b * CH + j, :], we1c[:, :], ACT.Copy, scale=ewT[:, ds(h * CH + j, 1)])
                last.then_inc(slots_set, 1)

            def hidden(b, value, last):
                if last is not None:
                    act.wait_ge(pe_steps, last)
                for j in range(CH):
                    act.wait_ge(gathered[b * CH + j], value)
                    stand(act)
                    nc.scalar.activation(GE[:, b * CH + j, :], M[:, b * CH + j, :], ACT.Gelu).then_inc(tiles_ready, 1)

            prepare(0, 0)
            for b in range(2):
                act.wait_ge(tiles_ready, 5 * TILES + b * CH - CH) if b else None
                prepare(b + 1, 1 - b) if b == 0 else None
                hidden(b, 80 * half + 32, None)
            act.wait_ge(tiles_ready, 5 * TILES + 2 * CH)
            prepare(2, 0)
            with act.Fori(1, half - 1) as i:
                for b in range(2):
                    last = act.value_load(tab_last[0:1, ds(i * 2 * CH + ((b - 1) * CH - 1), 1)], min_val=0, max_val=STEPS - 1)
                    act.wait_ge(tiles_ready, i * 2 * CH + (5 * TILES + b * CH))
                    stand(act)
                    prepare(i * 2 + (b + 1), 1 - b)
                    hidden(b, i * 32 + (80 * half + 32), last + (CREDIT + STEPS * 5 + 1))
            for b in range(2):
                h = CHUNKS - 2 + b
                last = act.value_load(tab_last[0:1, CH * (h - 1) - 1:CH * (h - 1)], min_val=0, max_val=STEPS - 1)
                if b == 0:
                    act.wait_ge(tiles_ready, 6 * TILES - 2 * CH)
                    prepare(CHUNKS - 1, 1)
                hidden(b, 112 * half, last + (CREDIT + STEPS * 5 + 1))
            def last_turn_too(i, tail):
                for b in range(2):
                    act.wait_ge(TR[b], i + 1 + at(6, "tr"))
                    act.wait_ge(MMB[b], i + at(6, "mmb"))
                    stand(act)
                    nc.scalar.activation(HT[:, b, :], ps[0][:, :], ACT.Copy)
                    nc.scalar.activation(AG[:, b, :], ps[1][:, :], ACT.Copy).then_inc(HT_[b], 1)
                    act.wait_ge(MMA[b], i + 1 + at(6, "mma"))
                    stand(act)
                    nc.scalar.activation(T1[:, b, :], ps[2 + b][:, :], ACT.Copy).then_inc(AT[b], 1)
                    act.wait_ge(MMB[b], i + 1 + at(6, "mmb"))
                    act.wait_ge(MMC[b], i + at(6, "mmc"))
                    stand(act)
                    nc.scalar.activation(T2[:, b, :], ps[4 + b][:, :], ACT.Gelu, bias=bu1col[:, 0:1]).then_inc(GL[b], 1)
                    act.wait_ge(Z_[b], i + 1 + at(6, "z"))
                    act.wait_ge(OUT[b], i + at(6, "out"))
                    stand(act)
                    for j in range(Q4):
                        last = nc.scalar.activation(q(HO[:, b, :])[:, j, :], q(Z[:, b, :])[:, j, :], ACT.Identity,
                                                    scale=SC[:, b, j:j + 1], bias=BI[:, b, j:j + 1])
                    last.then_inc(NRM[b], 1)
                    act.wait_ge(OUT[b], i + 1 + at(6, "out"))
                    g = i * 2 + b
                    if not (tail and b):
                        rows_out = out[0:(GROUPS - 1) * 512].rearrange("(g j p) d -> g p j d", j=Q4, p=P)
                        act.dma_start(rows_out[g], q(OB[:, b, :])).then_inc(ST_[b], 16)
                        continue
                    r0 = (GROUPS - 1) * 512
                    nb, rest = divmod(NODES - r0, P)
                    act.dma_start(out[r0:r0 + nb * P].rearrange("(j p) d -> p j d", p=P),
                                  q(OB[:, b, :])[:, 0:nb, :]).then_inc(ST_[b], 16)
                    act.dma_start(out[r0 + nb * P:NODES], q(OB[:, b, :])[0:rest, nb, :]).then_inc(ST_[b], 16)

            with act.Fori(0, TURNS - 1) as i:
                last_turn_too(i, False)
            last_turn_too(TURNS - 1, True)
            act.wait_ge(ST_[0], 16 * TURNS + at(6, "st"))
            act.wait_ge(ST_[1], 16 * (TURNS + 1) + at(6, "st"))

        @block.tensor
        def _(pe):
            mm = nc.tensor.matmul
            pe.sem_inc(pe_steps, CREDIT)
            pe.wait_ge(s_cv, 4)
            pe.wait_ge(s_w, 16 * NLOADS)
            for h in range(2):
                last = nc.tensor.transpose(ps[6][:, h * P:(h + 1) * P], wl[:, h * P:(h + 1) * P], ident[:, :])
            last.then_inc(s_wt, 1)
            for k in range(2):
                last = mm(ps[k][:, 0:BLOCKS], zero_h[:, :], oh_bk[:, 0, :], start=True, stop=False, skip_group_check=True)
            with pe.Fori(0, TILES // 2) as i:
                for c in range(2):
                    pe.wait_ge(s_oh, i * 2 + (c + 1))
                    for k in range(2):
                        last = mm(ps[k][:, 0:BLOCKS], oh_lo[:, 2 * c + k, :], oh_hi[:, 2 * c + k, :],
                                  start=False, stop=False, skip_group_check=True)
                    last.then_inc(s_hist, 1)
            pe.wait_ge(s_deg, 1)
            for k in range(Q4):
                last = mm(ps[2][0:BC, k:k + 1], deg[:, k * BC:(k + 1) * BC], ones[:, 0:1], start=True, stop=True)
            last.then_inc(s_cnt, 1)
            pe.wait_ge(s_cntc, 1)
            mm(ps[3][0:BC, 0:Q4], upper[0:BC, 0:BC], cnt[:, :], start=True, stop=False)
            mm(ps[3][0:BC, 0:Q4], ones[0:BC, 0:BC], cum[:, :], start=False, stop=True).then_inc(s_cum, 1)
            pe.wait_ge(s_diag, 1)
            for k in range(2):
                for c in range(Q4):
                    last = mm(ps[4 + k][:, c * BC:(c + 1) * BC], ones[0:BC, :], diag[:, c, :],
                              start=(c == 0), stop=False, skip_group_check=True)
            last.then_inc(s_base, 1)
            with pe.Fori(0, TILES // (2 * CH)) as i:
                for c in range(2 * CH):
                    bank = ps[4 + c % 2][:, 0:BLOCKS]
                    pe.wait_ge(s_rk, i * 2 * CH + (c + 1))
                    pe.wait_ge(s_rr, i * 2 * CH + (c + 1))
                    mm(bank, ones_h[:, :], oh_bk[:, (c - 1) % CH, :], start=False, stop=False, skip_group_check=True)
                    mm(bank, lower_h[:, :], oh_bk[:, (c - 2) % CH, :], start=False, stop=False, skip_group_check=True)
                    mm(bank, upper_h[:, :], oh_bk[:, c % CH, :], start=False, stop=False, skip_group_check=True).then_inc(s_rank, 1)
            n = 0
            for kind in range(5):
                w = TABW[kind]
                if kind >= 2:
                    pe.wait_ge(s_tabr, kind - 1)
                for c in range(Q4):
                    pe.wait_ge(s_ge, n + 1)
                    n += 1
                    last = mm(ps[2 + kind % 2][:, 0:w], ones[0:BC, :], ge[:, 0:w], start=(c == 0), stop=(c == Q4 - 1))
                    last.then_inc(s_tabm, 1)
            for k, t in enumerate((rdeg, deg)):
                for c in range(Q4):
                    last = nc.tensor.transpose(ps[k][0:BC, c * P:(c + 1) * P], t[:, c * BC:(c + 1) * BC], ident[:, :])
            last.then_inc(s_dt, 1)
            def block_products(bank, lhs, w):
                for j in range(Q4):
                    last = mm(q(bank[:, :])[:, j, :], lhs[:, j, :], w, start=True, stop=True)
                return last

            def turn_rows(bank, src_):
                for j in range(Q4):
                    last = nc.tensor.transpose(q(bank[:, :])[:, j, :], src_[:, j, :], ident[:, :])
                return last

            def dense_table(d, w):
                with pe.Fori(0, TURNS) as i:
                    for b in range(2):
                        pe.wait_ge(OUT[b], i + (at(d, "out") + 1))
                        pe.wait_ge(HT_[b], i + at(d, "ht"))
                        turn_rows(ps[b], q(HO[:, b, :])).then_inc(TR[b], 1)
                        pe.wait_ge(HT_[b], i + (at(d, "ht") + 1))
                        pe.wait_ge(GL[b], i + at(d, "gl"))
                        if d < 2:
                            block_products(ps[2 + b], q(HT[:, b, :]), w).then_inc(MM[b], 1)
                            continue
                        pe.wait_ge(EV[b], i + at(2, "ev"))
                        for j in range(Q4):
                            mm(q(ps[2 + 2 * b][:, :])[:, j, :], q(HT[:, b, :])[:, j, :], wlT[:, 0, :], start=True, stop=True)
                            o = q(ps[3 + 2 * b][:, :])[:, j, :]
                            mm(o, q(HT[:, b, :])[:, j, :], wlT[:, 1, :], start=True, stop=False)
                            last = mm(o, ones[0:1, :], bias[:, 2, :], start=False, stop=True)
                        last.then_inc(MM[b], 1)

            pe.wait_ge(s_dc, 1)
            dense_table(0, w1[:, :])
            for n in range(3 * Q4):
                pe.wait_ge(s_ec, n + 1)
                if n >= 2:
                    pe.wait_ge(s_er, n - 1)
                k, c = divmod(n, Q4)
                nc.tensor.transpose(ps[6 + n % 2][:, 0:BC], e_f[:, :], ident[0:BC, 0:BC]).then_inc(s_et, 1)

            def walk(ph):
                pe.wait_ge(s_rel, 1)
                with pe.Fori(0, SPINS) as i:
                    for j, t in enumerate(from_table(pe, tab_t, i * US, US, TILES - 1)):
                        s = i * US + j
                        slot = t % RING
                        ring = GE if ph == 5 else M
                        rows_ = ring[:, ds(slot, 1), :].rearrange("p o d -> p (o d)")
                        pe.wait_ge(tiles_ready, t + (TILES * ph + 1))
                        pe.wait_ge(oh_done, s + (WS * ph + 1))
                        pe.wait_ge(acc_steps, s + (CREDIT + STEPS * ph - 2))
                        mm(ps[j % 3][:, 0:P], OH[:, j % 3, :], rows_, start=True, stop=True).then_inc(pe_steps, 1)

            walk(0)
            dense_table(1, w2[:, :])
            walk(1)
            dense_table(2, None)
            walk(2)
            walk(3)
            with pe.Fori(0, TURNS) as i:
                for b in range(2):
                    pe.wait_ge(IN_[b], (i + 1) * 64 + at(4, "in"))
                    pe.wait_ge(HT_[b], i + at(4, "ht"))
                    pe.wait_ge(MEAN[b], i + at(4, "mean"))
                    turn_rows(ps[b], q(HB[:, b, :]))
                    turn_rows(ps[6 + b], q(IN[:, b, :])).then_inc(TR[b], 1)
                    pe.wait_ge(HT_[b], i + 1 + at(4, "ht"))
                    pe.wait_ge(MEAN[b], i + 1 + at(4, "mean"))
                    pe.wait_ge(HID[1 - b], i + b + at(4, "hid"))
                    for h in range(2):
                        mm(ps[2 + h][:, :], ws1[:, h * P:(h + 1) * P], HT[:, b, :], start=True, stop=False)
                        last = mm(ps[2 + h][:, :], wn1[:, h * P:(h + 1) * P], RB[:, b, :], start=False, stop=True)
                    last.then_inc(MMA[b], 1)
                    pe.wait_ge(HID[b], i + 1 + at(4, "hid"))
                    pe.wait_ge(OUT[1 - b], i + b + at(4, "out"))
                    pe.wait_ge(Z_[1 - b], i + b + at(4, "z"))
                    for j in range(Q4):
                        for k in range(2):
                            o = q(ps[4 + k][:, :])[:, j, :]
                            for h, t in enumerate((T1, T2)):
                                last = mm(o, q(t[:, b, :])[:, j, :], w42[:, h, k, :], start=(h == 0), stop=(h == 1 and k == 0))
                        last = mm(o, ones[0:1, :], bias[:, 3, :], start=False, stop=True)
                    last.then_inc(MM[b], 1)
            walk(4)
            with pe.Fori(0, TURNS) as i:
                for b in range(2):
                    pe.wait_ge(OUT[b], i + 1 + at(5, "out"))
                    pe.wait_ge(HT_[b], i + at(5, "ht"))
                    turn_rows(ps[b], q(HO[:, b, :])).then_inc(TR[b], 1)
                    pe.wait_ge(HT_[b], i + 1 + at(5, "ht"))
                    pe.wait_ge(EV[1 - b], i + b + at(5, "ev"))
                    for j in range(Q4):
                        o = ps[4 + j // 2][:, (j % 2) * 256:(j % 2) * 256 + 256]
                        mm(o, q(HT[:, b, :])[:, j, :], we1[:, :, :].rearrange("p k n -> p (k n)"), start=True, stop=False)
                        last = mm(o, ones[0:1, :], bz5, start=False, stop=True)
                    last.then_inc(MM[b], 1)
            walk(5)
            with pe.Fori(0, TURNS) as i:
                for b in range(2):
                    pe.wait_ge(IN_[b], (i + 1) * 64 + at(6, "in"))
                    pe.wait_ge(HT_[1 - b], i + b + at(6, "ht"))
                    turn_rows(ps[0], q(HB[:, b, :]))
                    turn_rows(ps[1], q(IN[:, b, :])).then_inc(TR[b], 1)
                    pe.wait_ge(HT_[b], i + 1 + at(6, "ht"))
                    pe.wait_ge(AT[b], i + at(6, "at"))
                    mm(ps[2 + b][:, :], we2[:, :], AG[:, b, :], start=True, stop=False)
                    mm(ps[2 + b][:, :], bias[:, 5, :], RB[0:1, b, :], start=False, stop=True).then_inc(MMA[b], 1)
                    pe.wait_ge(HT_[b], i + 1 + at(6, "ht"))
                    pe.wait_ge(AT[b], i + 1 + at(6, "at"))
                    pe.wait_ge(GL[b], i + at(6, "gl"))
                    mm(ps[4 + b][:, :], wu1[:, 0, :], HT[:, b, :], start=True, stop=False)
                    mm(ps[4 + b][:, :], wu1[:, 1, :], T1[:, b, :], start=False, stop=True).then_inc(MMB[b], 1)
                    pe.wait_ge(GL[b], i + 1 + at(6, "gl"))
                    pe.wait_ge(Z_[b], i + at(6, "z"))
                    for j in range(Q4):
                        o = q(ps[6 + b][:, :])[:, j, :]
                        mm(o, q(T2[:, b, :])[:, j, :], wu2[:, :], start=True, stop=False)
                        last = mm(o, ones[0:1, :], bias[:, 6, :], start=False, stop=True)
                    last.then_inc(MMC[b], 1)

        @block.vector
        def _(dve):
            v = nc.vector
            chain = Chain(dve, link_v)
            link = chain.link
            v.memset(oh_bk[:], 0.0)
            v.memset(bz[:], 0.0)
            v.memset(dhi[:, TILES:TILES + 1], 0.0)
            for k in range(2):
                v.memset(pack[k][:], 0)
            dve.sem_inc(acc_steps, CREDIT)
            dve.wait_ge(s_const, 6)
            v.tensor_copy(iota_f[:], iota_i[:]).then_inc(s_cv, 1)
            v.tensor_copy(iota_h[:], iota_i[:, 0:BLOCKS]).then_inc(s_cv, 1)
            v.tensor_copy(part_f[:], part_i[:])
            v.tensor_copy(upper_h[:], upper[:])
            v.tensor_copy(ones_h[:], ones[:])
            link(v.memset(zero_h[:], 0.0))
            v.tensor_tensor(lower_h[:], ones_h[:], upper_h[:], ALU.subtract).then_inc(s_cv, 1)
            dve.wait_ge(s_cv, 3)
            dve.wait_ge(s_load, 96)
            for t, lo, hi in ((src_o, slo, shi), (dst_o, dlo, dhi)):
                link(v.tensor_scalar(cut_i[:], t[:], P - 1, None, ALU.bitwise_and))
                link(v.tensor_copy(lo[:], cut_i[:]))
                link(v.tensor_scalar(cut_i[:], t[:], 7, None, ALU.logical_shift_right))
                link(v.tensor_copy(hi[:, 0:TILES], cut_i[:]))
            dve.wait_ge(s_w, 16 * NLOADS)
            v.tensor_copy(bz[:, 0, P:2 * P], bias[:, 3, :])
            v.tensor_copy(bz[:, 2, P:2 * P], bias[:, 2, :])
            v.tensor_copy(bz[:, 1, P:2 * P], bias[:, 4, :]).then_inc(s_cv, 1)
            dve.wait_ge(s_wt, 1)
            v.tensor_copy(wlT[:, 0, :], ps[6][:, P:2 * P])
            v.tensor_copy(wlT[:, 1, :], ps[6][:, 0:P])
            for t4, t in ((b2x4, b2bc), (gam4, gam), (bet4, bet)):
                for j in range(Q4):
                    last = v.tensor_copy(q(t4[:, :])[:, j, :], t[:, :])
            link(last)


            def hist_column(i, c, wait):
                if wait is not None:
                    dve.wait_ge(s_hist, wait)
                col = i * 2 + c
                for k, (lo, hi) in enumerate(((slo, shi), (dlo, dhi))):
                    v.tensor_scalar(oh_lo[:, 2 * c + k, :], iota_h[:, 0:P], lo[:, ds(col, 1)], None, ALU.is_equal)
                    last = v.tensor_scalar(oh_hi[:, 2 * c + k, :], iota_h[:, :], hi[:, ds(col, 1)], None, ALU.is_equal)
                last.then_inc(s_oh, 1)

            hist_column(0, 0, None)
            hist_column(0, 1, None)
            with dve.Fori(1, TILES // 2) as i:
                for c in range(2):
                    hist_column(i, c, i * 2 + (c - 1))
            dve.wait_ge(s_hist, TILES)
            v.tensor_copy(deg[:, :], ps[1][:, 0:BLOCKS]).then_inc(s_deg, 1)
            link(v.tensor_scalar(nsrc[:, :], ps[0][:, 0:BLOCKS], 1.0, None, ALU.max))
            link(v.tensor_scalar(ndst[:, :], deg[:, :], 1.0, None, ALU.max))
            link(v.reciprocal(rdeg[:, :], ndst[:, :]))
            dve.sem_inc(s_deg1, 1)
            dve.wait_ge(s_cnt, 1)
            link(v.tensor_copy(cnt[:, :], ps[2][0:BC, 0:Q4]))
            link(v.memset(cum[:, 0:1], 0.0))
            for k in range(1, Q4):
                link(v.tensor_tensor(cum[:, k:k + 1], cum[:, k - 1:k], cnt[:, k - 1:k], ALU.add))
            dve.sem_inc(s_cntc, 1)
            dve.wait_ge(s_cum, 1)
            link(v.tensor_copy(before[:, :], ps[3][0:BC, 0:Q4]))
            for k in range(Q4):
                last = v.tensor_scalar(diag[:, k, :], ident[0:BC, 0:BC], before[:, k:k + 1], None, ALU.mult)
            last.then_inc(s_diag, 1)
            link(v.tensor_copy(before_i[:, :], before[:, :]))
            link(v.tensor_scalar(before_i[:, :], before_i[:, :], 7, None, ALU.logical_shift_right))
            link(v.tensor_copy(first[:, :], before_i[:, :]))
            for k in range(Q4):
                link(v.tensor_scalar(blk[:, k:k + 1], part_f[0:BC, :], float(k * BC), None, ALU.add))
            link(v.tensor_tensor(start[:, :], first[:, :], blk[:, :], ALU.add))

            def rank_onehot(col, c):
                v.tensor_scalar(oh_bk[:, c % CH, :], iota_h[:, :], dhi[:, ds(col, 1)], None, ALU.is_equal).then_inc(s_rk, 1)

            rank_onehot(0, 0)
            dve.sem_inc(s_rr, 2)
            with dve.Fori(0, TILES // (2 * CH)) as i:
                for c in range(2 * CH):
                    b = c // CH
                    rank_onehot(i * 2 * CH + (c + 1), c + 1)
                    dve.wait_ge(s_rank, i * 2 * CH + (c + 1))
                    v.tensor_tensor_reduce(junk[:, c % 2, :], ps[4 + c % 2][:, 0:BLOCKS], oh_bk[:, c % CH, :], 1.0, 0.0,
                                           ALU.mult, ALU.add, posf[:, c:c + 1]).then_inc(s_rr, 1)
                    if c % CH == CH - 1:
                        dve.wait_ge(s_rr, i * 2 * CH + (c + 1 + 2))
                        dve.wait_ge(s_scat[b], i * (16 * CH))
                        stand(dve)
                        for f, t in enumerate((src_o[:, :], dst_o[:, :], ew_o[:, :].bitcast(I32))):
                            v.tensor_copy(pack[b][:, :, f], t[:, ds(i * 2 * CH + b * CH, CH)])
                        v.tensor_copy(pos_i[b][:, :], posf[:, b * CH:(b + 1) * CH]).then_inc(s_pack[b], 1)

            n = 0
            for kind in range(5):
                lo = 512 * (kind % 2) if kind < 4 else 0
                for c in range(Q4):
                    if n:
                        dve.wait_ge(s_tabm, n)
                    n += 1
                    col = (first if kind == 4 else start)[:, c:c + 1]
                    v.tensor_scalar(ge[:, 0:TABW[kind]], iota_f[0:BC, lo:lo + TABW[kind]], col, None,
                                    ALU.is_equal if kind in (2, 3) else ALU.is_ge).then_inc(s_ge, 1)
                dve.wait_ge(s_tabm, n)
                got = ps[2 + kind % 2]
                if kind < 2:
                    ins = v.tensor_scalar(b_row[:, lo:lo + TABW[kind]], got[:, 0:TABW[kind]], -1.0, None, ALU.add)
                elif kind < 4:
                    ins = v.tensor_scalar(keep[:, lo:lo + TABW[kind]], got[:, 0:TABW[kind]], -1.0, 1.0, ALU.mult, ALU.add)
                else:
                    ins = v.scalar_tensor_tensor(ls_row[:, :], got[0:1, 0:TILES], -1.0, iota_f[0:1, 0:TILES], ALU.add, ALU.add)
                chain.link(ins)
                dve.sem_inc(s_tabr, 1)
            link(v.memset(keep[:, STEPS:STEPS + 1], 0.0))
            link(v.tensor_tensor(t_row[:, :], iota_f[0:1, :], b_row[0:1, :], ALU.subtract))
            link(v.scalar_tensor_tensor(dest_f[:, 0:STEPS], t_row[:, 0:STEPS], float(BLOCKS), keep[0:1, 1:STEPS + 1], ALU.add, ALU.mult))
            link(v.tensor_tensor(dest_f[:, 0:STEPS], dest_f[:, 0:STEPS], b_row[0:1, 0:STEPS], ALU.add))
            v.tensor_copy(tab_t[:, 0:STEPS], t_row[:, 0:STEPS])
            v.tensor_copy(tab_dest[:, 0:STEPS], dest_f[:, 0:STEPS])
            link(v.tensor_copy(tab_last[:, :], ls_row[:, :]))
            link(v.tensor_scalar(b_row[:, :], b_row[:, :], float(P), None, ALU.mult))
            dve.wait_ge(s_dt, 1)
            for k in range(2):
                last = v.tensor_copy(OB[0:BC, k, :], ps[k][0:BC, :])
            last.then_inc(s_dc, 1)

            def norm(b, src_):
                for j in range(Q4):
                    last = v.bn_stats(ST[:, b, j, :], src_[:, j, :])
                link(last)
                stand(dve)
                for j in range(Q4):
                    last = v.bn_aggr(MV[:, b, j, :], ST[:, b, j, :])
                return last

            with dve.Fori(0, TURNS) as i:
                chain.turn(i, 2 * 1)
                for b in range(2):
                    dve.wait_ge(IN_[b], i * 16 + 16 + at(0, "in"))
                    dve.wait_ge(OUT[b], i + at(0, "out"))
                    norm(b, q(XB[:, b, :])).then_inc(STAT[b], 1)
                chain.over(TURNS)

            dve.wait_ge(s_el, 64)
            for n in range(3 * Q4):
                k, c = divmod(n, Q4)
                part = slice(c * BC, (c + 1) * BC)
                if n:
                    dve.wait_ge(s_et, n)
                field = e_in[:, c, :].rearrange("t (p f) -> t p f", f=4)[:, :, k]
                v.tensor_copy(e_f[:, :], field.bitcast(F32) if k == 2 else field).then_inc(s_ec, 1)
                dve.wait_ge(s_et, n + 1)
                got = ps[6 + n % 2][:, 0:BC]
                if k == 0:
                    v.tensor_copy(srcT[:, part], got).then_inc(s_er, 1)
                elif k == 1:
                    v.tensor_copy(dstT[:, part], got)
                    v.tensor_copy(dstF[:, part], got).then_inc(s_er, 1)
                else:
                    v.tensor_copy(ewT[:, part], got).then_inc(s_er, 1)
            dve.wait_ge(s_er, 3 * Q4)
            link(v.memset(dstrel[:, STEPS:WS], -1.0))
            with dve.Fori(0, SPINS) as i:
                for j, t in enumerate(from_table(dve, tab_t, i * US, US, TILES - 1)):
                    v.tensor_tensor(dstrel[:, ds(i * US + j, 1)], dstF[:, ds(t, 1)], b_row[:, ds(i * US + j, 1)], ALU.subtract)
            link(v.memset(ACC[:, :, :], 0.0))
            dve.sem_inc(s_rel, 1)

            def walk(ph):
                def onehot(s, k):
                    dve.wait_ge(pe_steps, s + (CREDIT + STEPS * ph - 2))
                    v.tensor_scalar(OH[:, k % 3, :], iota_f[:, 0:P], dstrel[:, ds(s, 1)], None, ALU.is_equal).then_inc(oh_done, 1)

                for k in range(LEAD):
                    onehot(k, k)
                with dve.Fori(0, SPINS) as i:
                    for j in range(US):
                        s = i * US + j
                        onehot(i * US + (j + LEAD), j + LEAD)
                        dve.wait_ge(pe_steps, s + (CREDIT + STEPS * ph + 1))
                        dve.wait_ge(acc_steps, s + (CREDIT + STEPS * ph))
                        dve.wait_ge(out_done[j % SUMS], i * (16 * US // SUMS) + (16 * LAPS * ph + 16 * (j // SUMS)))
                        v.scalar_tensor_tensor(ACC[:, j % SUMS, :], ACC[:, (j - 1) % SUMS, :], keep[:, ds(s, 1)], ps[j % 3][:, 0:P],
                                               ALU.mult, ALU.add).then_inc(acc_steps, 1)

            def per_block(b, bank, scale, other, i):
                for j in range(Q4):
                    last = v.scalar_tensor_tensor(q(Z[:, b, :])[:, j, :], q(bank)[:, j, :],
                                                  scale[:, ds((i * 2 + b) * Q4 + j, 1)], other(j), ALU.mult, ALU.add)
                return last

            dve.wait_ge(s_pow, 2)
            walk(0)
            with dve.Fori(0, TURNS) as i:
                for b in range(2):
                    dve.wait_ge(IN_[b], i * 16 + (at(1, "in") + 16))
                    dve.wait_ge(OUT[b], i + at(1, "out"))
                    per_block(b, IN[:, b, :], ndst, lambda j: b1bc[:, :], i).then_inc(Z_[b], 1)
            walk(1)
            with dve.Fori(0, TURNS) as i:
                chain.turn(i, 2 * 3)
                for b in range(2):
                    dve.wait_ge(IN_[b], i * 32 + (at(2, "in") + 32))
                    dve.wait_ge(OUT[b], i + at(2, "out"))
                    link(per_block(b, IN[:, b, :], ndst, lambda j: q(XB[:, b, :])[:, j, :], i))
                    link(v.tensor_tensor(Z[:, b, :], Z[:, b, :], b2x4[:, :], ALU.add))
                    norm(b, q(Z[:, b, :])).then_inc(STAT[b], 1)
                    dve.wait_ge(MM[b], i + (at(2, "mm") + 1))
                    dve.wait_ge(ST_[b], i * 32 + at(2, "st"))
                    stand(dve)
                    v.tensor_tensor(T2[:, b, :], ps[3 + 2 * b][:, :], Z[:, b, :], ALU.add).then_inc(EV[b], 1)
                chain.over(TURNS)
            walk(2)
            with dve.Fori(0, TURNS) as i:
                chain.turn(i, 2 * 2)
                for b in range(2):
                    dve.wait_ge(IN_[b], i * 32 + (at(3, "in") + 32))
                    dve.wait_ge(OUT[b], i + at(3, "out"))
                    dve.wait_ge(ST_[b], i * 32 + at(3, "st"))
                    link(per_block(b, IN[:, b, :], rdeg, lambda j: q(XB[:, b, :])[:, j, :], i))
                    norm(b, q(Z[:, b, :])).then_inc(STAT[b], 1)
                chain.over(TURNS)
            walk(3)
            with dve.Fori(0, TURNS) as i:
                for b in range(2):
                    dve.wait_ge(IN_[b], i * 64 + 64 + at(4, "in"))
                    dve.wait_ge(TR[b], i + (at(4, "tr") + 1))
                    v.tensor_tensor(RB[:, b, :], ps[6 + b][:, :], RB[:, b, :], ALU.mult).then_inc(MEAN[b], 1)
                    dve.wait_ge(MM[b], i + 1 + at(4, "mm"))
                    dve.wait_ge(ST_[b], i * 32 + at(4, "st"))
                    v.tensor_tensor(Z[:, b, :], ps[5][:, :], XB[:, b, :], ALU.add).then_inc(Z_[b], 1)
            walk(4)
            with dve.Fori(0, TURNS) as i:
                chain.turn(i, 2 * 2)
                for b in range(2):
                    dve.wait_ge(IN_[b], i * 32 + 32 + at(5, "in"))
                    dve.wait_ge(OUT[b], i + at(5, "out"))
                    dve.wait_ge(ST_[b], i * 64 + at(5, "st"))
                    link(per_block(b, IN[:, b, :], rdeg, lambda j: q(XB[:, b, :])[:, j, :], i))
                    norm(b, q(Z[:, b, :])).then_inc(STAT[b], 1)
                    dve.wait_ge(MM[b], i + 1 + at(5, "mm"))
                    for t, n in ((T1, 0), (T2, 1)):
                        for k in range(2):
                            last = v.tensor_copy(q(t[:, b, :])[:, 2 * k:2 * k + 2, :], q(ps[4 + k][:, :])[:, n:4:2, :])
                    last.then_inc(EV[b], 1)
                chain.over(TURNS)
            walk(5)
            with dve.Fori(0, TURNS) as i:
                chain.turn(i, 2 * 4)
                for b in range(2):
                    dve.wait_ge(IN_[b], i * 64 + 64 + at(6, "in"))
                    dve.wait_ge(MMC[b], i + 1 + at(6, "mmc"))
                    dve.wait_ge(NRM[b], i + at(6, "nrm"))
                    v.tensor_tensor(XB[:, b, :], XB[:, b, :], bet4[:, :], ALU.add)
                    link(v.tensor_tensor(Z[:, b, :], HB[:, b, :], ps[6 + b][:, :], ALU.add))
                    norm(b, q(Z[:, b, :])).then_inc(STAT[b], 1)
                    dve.wait_ge(NRM[b], i + 1 + at(6, "nrm"))
                    dve.wait_ge(ST_[b], i * 16 + at(6, "st"))
                    link(v.tensor_tensor(OB[:, b, :], HO[:, b, :], gam4[:, :], ALU.mult))
                    link(v.tensor_tensor(OB[:, b, :], OB[:, b, :], XB[:, b, :], ALU.add))
                    dve.sem_inc(OUT[b], 1)
                chain.over(TURNS)


_INS = ["x", "src", "dst", "edge_weight", "L0_gnn_W1", "L0_gnn_b1", "L0_gnn_W2", "L0_gnn_b2", "L1_gnn_W",
        "L1_gnn_b", "L2_gnn_W_self1", "L2_gnn_W_neigh1", "L2_gnn_b1", "L2_gnn_W_self2", "L2_gnn_W_neigh2",
        "L2_gnn_b2", "L3_gnn_We1", "L3_gnn_be1", "L3_gnn_We2", "L3_gnn_be2", "L3_gnn_Wu1", "L3_gnn_bu1",
        "L3_gnn_Wu2", "L3_gnn_bu2", "L3_gnn_gamma", "L3_gnn_beta"]


def kernel(**inputs):
    import numpy as _np
    import concourse.bacc as _bacc
    from concourse.bass_utils import run_bass_kernel_spmd as _run

    nc = _bacc.Bacc("TRN2", target_bir_lowering=False, num_devices=1)
    arrays, args = {}, {}
    for name in _INS:
        arr = _np.ascontiguousarray(inputs[name])
        arrays[f"in_{name}"] = arr
        args[name] = nc.dram_tensor(f"in_{name}", arr.shape, mybir.dt.from_np(arr.dtype), kind="ExternalInput").ap()
    out = nc.dram_tensor("out_0", (NODES, P), F32, kind="ExternalOutput").ap()
    program(nc, args, out)
    r = _run(nc, [arrays], core_ids=[0])
    return r.results[0]["out_0"]
```

```python
from contextlib import ExitStack

import concourse.bass as bass
from concourse import mybir

F32 = mybir.dt.float32
F16 = mybir.dt.float16
I32 = mybir.dt.int32
ALU = mybir.AluOpType
ACT = mybir.ActivationFunctionType
ds = bass.ds

P = 128
NODES = 50000
EDGES = 50000
BLOCKS = 392
TILES = 392
NP = BLOCKS * P
PAD_NODE = NP - 1
STEPS = TILES + BLOCKS - 1
US = 27
SPINS = STEPS // US
SUMS = 9
LAPS = STEPS // SUMS
RING = 14
CH = 7
CHUNKS = TILES // CH
NLOADS = 23
TABW = [512, STEPS + 2 - 512, 512, STEPS + 2 - 512, TILES]
LEAD = 2
WS = STEPS + LEAD
Q4 = 4
BC = BLOCKS // Q4
GROUPS = BLOCKS // Q4
TURNS = GROUPS // 2
EPS = 1e-5
CREDIT = 9
assert SPINS * US == STEPS and NP >= NODES and CHUNKS % 2 == 0


class Chain:

    def __init__(self, eng, sem):
        self.eng, self.sem, self.done, self.i, self.k, self.per = eng, sem, 0, None, 0, 0

    def turn(self, i, per, first=0):
        self.i, self.k, self.per, self.first = i, 0, per, first

    def over(self, n):
        assert self.k == self.per, (self.k, self.per)
        self.done += (n - self.first) * self.per
        self.i = None

    def link(self, ins):
        ins.then_inc(self.sem, 1)
        if self.i is None:
            self.done += 1
            self.eng.wait_ge(self.sem, self.done)
        else:
            self.k += 1
            self.eng.wait_ge(self.sem, self.i * self.per + (self.done - self.first * self.per + self.k))


def staggered(eng, parts, chain=None, links=0):
    most = max(lag for lag, _ in parts)
    first = max(1, (most + 1) // 2)
    for n in range(2 * first):
        for lag, do in parts:
            if n >= lag:
                do(*divmod(n - lag, 2))
    with eng.Fori(first, TURNS) as i:
        if chain:
            chain.turn(i, 2 * links, first)
        for b in range(2):
            for lag, do in parts:
                back, parity = divmod(b - lag, 2)
                do(i + back, parity)
        if chain:
            chain.over(TURNS)
    for n in range(GROUPS, GROUPS + most):
        for lag, do in parts:
            if n - lag < GROUPS:
                do(*divmod(n - lag, 2))


def program(nc, a, out):
    with ExitStack() as ctx:
        def sb(name, shape, dt=F32):
            return ctx.enter_context(nc.sbuf_tensor(name, shape, dt))

        def sem(name):
            return ctx.enter_context(nc.semaphore(name))

        def pair(name):
            return [sem(f"{name}{k}") for k in range(2)]

        def dram(name, shape, dt=F32):
            return nc.dram_tensor(name, shape, dt).ap()

        edges = dram("edges_by_block", [NP, 4], I32)
        x_pad = dram("x_pad", [NP, P])
        agg = dram("agg", [BLOCKS + STEPS, P, P])
        tabs = [dram("table_a", [NP, P]), dram("table_b", [NP, P])]
        q_tab = dram("table_dst", [NP, P])
        h5_d = dram("h5_rows", [NP, P])
        state = dram("state", [NP, P])
        rdeg_row = dram("rdeg_row", [BLOCKS, P])
        deg_row = dram("deg_row", [BLOCKS, P])

        def rows(t, g):
            return t.rearrange("(g j p) d -> g p j d", j=Q4, p=P)[g]

        def sums(g):
            return agg.rearrange("b f n -> f b n")[:, ds(g * Q4, Q4), :]

        ident = sb("ident", [P, P]); ones = sb("ones", [P, P]); zero = sb("zero", [P, P])
        iota_i = sb("iota_i", [P, WS], I32); iota_f = sb("iota_f", [P, WS])
        iota_h = sb("iota_h", [P, BLOCKS], F16)
        upper = sb("upper", [P, P]); upper_h = sb("upper_h", [P, P], F16)
        lower_h = sb("lower_h", [P, P], F16); ones_h = sb("ones_h", [P, P], F16)
        zero_h = sb("zero_h", [P, P], F16)
        part_i = sb("part_i", [P, 1], I32); part_f = sb("part_f", [P, 1])
        src_o = sb("src_o", [P, TILES], I32); dst_o = sb("dst_o", [P, TILES], I32)
        ew_o = sb("ew_o", [P, TILES])
        cut_i = sb("cut_i", [P, TILES], I32)
        slo = sb("slo", [P, TILES]); shi = sb("shi", [P, TILES])
        dlo = sb("dlo", [P, TILES]); dhi = sb("dhi", [P, TILES + 1])
        oh_lo = sb("oh_lo", [P, 4, P], F16); oh_hi = sb("oh_hi", [P, 4, BLOCKS], F16)
        oh_bk = sb("oh_bk", [P, CH, BLOCKS], F16)
        junk = sb("junk", [P, 2, BLOCKS])
        deg = sb("deg", [P, BLOCKS]); nsrc = sb("nsrc", [P, BLOCKS])
        ndst = sb("ndst", [P, BLOCKS]); rdeg = sb("rdeg", [P, BLOCKS])
        cnt = sb("cnt", [BC, Q4]); cum = sb("cum", [BC, Q4]); before = sb("before", [BC, Q4])
        before_i = sb("before_i", [BC, Q4], I32); first = sb("first", [BC, Q4])
        start = sb("start", [BC, Q4]); diag = sb("diag", [BC, Q4, BC]); blk = sb("blk", [BC, Q4])
        ge = sb("ge", [BC, 512])
        b_row = sb("b_row", [P, WS]); keep = sb("keep", [P, WS]); t_row = sb("t_row", [1, WS])
        dest_f = sb("dest_f", [1, WS]); ls_row = sb("ls_row", [1, TILES])
        tab_t = sb("tab_t", [1, WS], I32); tab_dest = sb("tab_dest", [1, WS], I32)
        tab_last = sb("tab_last", [1, TILES], I32)
        posf = sb("posf", [P, 2 * CH])
        pos_i = [sb(f"pos_i{k}", [P, CH], I32) for k in range(2)]
        pack = [sb(f"pack{k}", [P, CH, 4], I32) for k in range(2)]
        e_in = sb("e_in", [BC, Q4, P * 4], I32); e_f = sb("e_f", [BC, P])
        srcT = sb("srcT", [P, TILES], I32); dstT = sb("dstT", [P, TILES], I32)
        dstF = sb("dstF", [P, TILES]); ewT = sb("ewT", [P, TILES])
        dstrel = sb("dstrel", [P, WS])
        six = [sb(f"six{k}", [P, CH], I32) for k in range(2)]
        dix = [sb(f"dix{k}", [P, CH], I32) for k in range(2)]
        M = sb("M", [P, RING, P]); GE = sb("GE", [P, RING, P])
        OH = sb("OH", [P, 3, P]); ACC = sb("ACC", [P, SUMS, P])
        w1 = sb("w1", [P, P]); w2 = sb("w2", [P, P])
        wl = sb("wl", [P, 2 * P]); wlT = sb("wlT", [P, 2, P])
        ws1 = sb("ws1", [P, 2 * P]); wn1 = sb("wn1", [P, 2 * P])
        w42 = sb("w42", [P, 2, 2, P])
        we1 = sb("we1", [P, 2, P]); we2 = sb("we2", [P, P])
        wu1 = sb("wu1", [P, 2, P]); wu2 = sb("wu2", [P, P])
        linb = sb("linb", [1, P])
        b1col = sb("b1col", [P, 2]); bu1col = sb("bu1col", [P, 1])
        b1bc = sb("b1bc", [P, P]); b2bc = sb("b2bc", [P, P]); we1c = sb("we1c", [P, P])
        gam = sb("gam", [P, P]); bet = sb("bet", [P, P])
        gam4 = sb("gam4", [P, 512]); bet4 = sb("bet4", [P, 512]); b2x4 = sb("b2x4", [P, 512])
        sb2x4 = sb("sb2x4", [P, 512]); be1x4 = sb("be1x4", [P, 512]); bu2x4 = sb("bu2x4", [P, 512])
        sb2bc = sb("sb2bc", [P, P]); be1bc = sb("be1bc", [P, P]); bu2bc = sb("bu2bc", [P, P])
        be2col = sb("be2col", [P, 1]); we2T = sb("we2T", [P, P]); wm = sb("wm", [P, P]); cm = sb("cm", [1, P])
        XS = sb("XS", [P, 2, 512])
        IN = sb("IN", [P, 2, 512]); XB = sb("XB", [P, 2, 512]); HB = sb("HB", [P, 2, 512])
        HT = sb("HT", [P, 2, 512]); Z = sb("Z", [P, 2, 512]); HO = sb("HO", [P, 2, 512])
        T1 = sb("T1", [P, 2, 512]); T2 = sb("T2", [P, 2, 512]); RB = sb("RB", [P, 2, 512])
        OB = sb("OB", [P, 2, 512]); AG = sb("AG", [P, 2, 512])
        MV = sb("MV", [P, 2, Q4, 2]); ST = sb("ST", [P, 2, Q4, 6])
        SC = sb("SC", [P, 2, Q4]); BI = sb("BI", [P, 2, Q4]); VE = sb("VE", [P, 2, Q4]); NM = sb("NM", [P, 2, Q4])
        mhalf = sb("mhalf", [P, BLOCKS])

        ps = [ctx.enter_context(nc.psum_tensor(f"ps{k}", [P, 512], F32)) for k in range(8)]

        def q(t):
            return t.rearrange("p (j d) -> p j d", j=Q4)

        s_const = sem("consts_made"); s_cv = sem("consts_cast"); s_load = sem("edges_loaded")
        s_pad = sem("padding_set"); s_w = sem("weights_loaded"); s_xp = sem("x_padded")
        s_w42 = sem("w_transposed"); s_split = sem("ids_split")
        s_oh = sem("hist_onehots"); s_hist = sem("hist_columns"); s_hz = sem("hist_cleared")
        s_deg = sem("degrees_read"); s_cnt = sem("block_counts"); s_cntc = sem("block_counts_read")
        s_cum = sem("before_counts"); s_deg1 = sem("degrees_clamped"); s_pow = sem("norms_made"); s_tabm = sem("table_products"); s_tabr = sem("table_reads")
        s_ge = sem("table_masks")
        s_diag = sem("diag_made"); s_base = sem("rank_bases"); s_rk = sem("rank_onehots")
        s_rank = sem("rank_products"); s_rr = sem("rank_reads"); s_pack = pair("rows_packed")
        s_scat = pair("rows_placed"); s_el = sem("sorted_loaded"); s_ec = sem("sorted_cast")
        s_et = sem("sorted_turned"); s_er = sem("sorted_read"); s_rel = sem("walk_ready")
        s_dt = sem("deg_turned"); s_dc = sem("deg_copied"); s_dr = sem("deg_rows_stored")
        s_wt = sem("lin_turned")
        pe_steps = sem("pe_steps"); acc_steps = sem("acc_steps"); oh_done = sem("onehots_done")
        tiles_ready = sem("tiles_ready"); idx_ready = sem("idx_ready")
        gathered = [sem(f"gathered{k}") for k in range(RING)]
        out_done = [sem(f"sum_written{k}") for k in range(SUMS)]
        slots_set = sem("slots_set"); gelu_own = sem("gelu_done")
        paced = sem("paced")
        link_v = sem("vector_link"); link_p = sem("pool_link")
        D = {w: pair(f"dense_{w}_") for w in "in stat coef out st mm z tr ht mean mma hid ev at mmb mmc gl nrm late".split()}
        IN_, STAT, COEF, OUT, ST_, MM, Z_, TR, HT_ = (D[w] for w in "in stat coef out st mm z tr ht".split())
        MEAN, MMA, HID, EV, AT, MMB, MMC, GL, NRM = (D[w] for w in "mean mma hid ev at mmb mmc gl nrm".split())
        ADDED, SUMMED, LATE, LSTORE = HID, AT, D["late"], MMC
        USES = {"in": [16, 16, 32, 32, 48, 32, 32], "late": [0, 0, 0, 0, 16, 0, 32], "mmc": [0, 0, 0, 0, 0, 32, 1],
                "st": [16, 16, 32, 32, 32, 32, 16], "hid": [0, 0, 1, 0, 1, 0, 1],
                "coef": [1, 0, 0, 0, 0, 0, 0], "stat": [1, 0, 1, 1, 0, 1, 1], "out": [1] * 7, "mm": [1, 1, 1, 0, 1, 1, 0],
                "z": [0, 1, 1, 1, 1, 1, 1], "tr": [1, 1, 1, 0, 1, 1, 1], "ht": [1, 1, 1, 0, 1, 1, 1],
                "ev": [0, 0, 1, 0, 0, 1, 0], "gl": [1, 1, 1, 0, 0, 1, 1], "mma": [0, 0, 0, 0, 1, 0, 0]}

        def at(d, w):
            return TURNS * sum(USES[w][:d]) if w in USES else 0

        block = ctx.enter_context(nc.Block())

        def from_table(eng, table, at_, n, most):
            return nc.values_load_multi_w_load_instructions(table[0:1, ds(at_, n)], engines=[eng.engine],
                                                            min_val=0, max_val=most)[1]

        def stand(eng):
            eng.sem_inc(paced, 1)

        def written(eng, ph):
            for k in range(SUMS):
                eng.wait_ge(out_done[k], 16 * LAPS * (ph + 1))

        def stored(eng, d):
            for k in range(2):
                eng.wait_ge(ST_[k], at(d + 1, "st"))
                if d == 5:
                    eng.wait_ge(LSTORE[k], at(6, "mmc"))

        @block.sync
        def _(sp):
            full = NP // P
            whole = EDGES // full
            sp.wait_ge(s_pad, 3)
            for t, name in ((src_o, "src"), (dst_o, "dst"), (ew_o, "edge_weight")):
                sp.dma_start(t[0:whole, :], a[name][0:whole * full].rearrange("(p c) -> p c", c=full)).then_inc(s_load, 16)
                sp.dma_start(t[whole:whole + 1, 0:EDGES - whole * full],
                             a[name][whole * full:EDGES].rearrange("(p c) -> p c", p=1)).then_inc(s_load, 16)
            sp.wait_ge(s_const, 3)
            sp.dma_start(x_pad[0:NODES].rearrange("(s b) d -> s (b d)", s=16),
                         a["x"].rearrange("(s b) d -> s (b d)", s=16)).then_inc(s_xp, 16)
            sp.dma_start(x_pad[NODES:NODES + P], zero[:, :]).then_inc(s_xp, 16)
            sp.dma_start(x_pad[NODES + P:NP], zero[0:NP - NODES - P, :]).then_inc(s_xp, 16)
            r1 = lambda v: v.rearrange("(o n) -> o n", o=1)
            bc = lambda v: v.rearrange("(o n) -> o n", o=1).broadcast_to([P, P])
            loads = [
                (w1[:, :], a["L0_gnn_W1"]), (w2[:, :], a["L0_gnn_W2"]), (wl[:, :], a["L1_gnn_W"]),
                (ws1[:, :], a["L2_gnn_W_self1"]), (wn1[:, :], a["L2_gnn_W_neigh1"]),
                (w42[:, :, 0, :], a["L2_gnn_W_neigh2"].rearrange("(h p) n -> p h n", h=2)),
                (w42[:, :, 1, :], a["L2_gnn_W_self2"].rearrange("(h p) n -> p h n", h=2)),
                (we1[:, :, :], a["L3_gnn_We1"][0:2 * P].rearrange("(h p) n -> p h n", h=2)),
                (we2[:, :], a["L3_gnn_We2"]),
                (wu1[:, :, :], a["L3_gnn_Wu1"].rearrange("(h p) n -> p h n", h=2)),
                (wu2[:, :], a["L3_gnn_Wu2"]),
                (linb[:, :], r1(a["L1_gnn_b"])),
                (sb2bc[:, :], bc(a["L2_gnn_b2"])), (be1bc[:, :], bc(a["L3_gnn_be1"])), (bu2bc[:, :], bc(a["L3_gnn_bu2"])),
                (be2col[:, :], a["L3_gnn_be2"].rearrange("(p o) -> p o", o=1)),
                (b1col[:, :], a["L2_gnn_b1"].rearrange("(h p) -> p h", h=2)),
                (bu1col[:, :], a["L3_gnn_bu1"].rearrange("(p o) -> p o", o=1)),
                (b1bc[:, :], bc(a["L0_gnn_b1"])), (b2bc[:, :], bc(a["L0_gnn_b2"])),
                (we1c[:, :], a["L3_gnn_We1"][2 * P:2 * P + 1].broadcast_to([P, P])),
                (gam[:, :], bc(a["L3_gnn_gamma"])), (bet[:, :], bc(a["L3_gnn_beta"])),
            ]
            assert len(loads) == NLOADS
            for dst_, src_ in loads:
                sp.dma_start(dst_, src_, allow_slow_non_contiguous=True).then_inc(s_w, 16)

            sp.wait_ge(s_xp, 48)
            with sp.Fori(0, TURNS) as i:
                for b in range(2):
                    sp.wait_ge(OUT[b], i + at(0, "out"))
                    sp.dma_start(q(XB[:, b, :]), rows(x_pad, 2 * i + b)).then_inc(IN_[b], 16)
            for k in range(2):
                sp.wait_ge(s_scat[k], 16 * TILES // 2)
            for k in range(Q4):
                sp.dma_start(e_in[:, k, :], edges.rearrange("(k t p) f -> k t (p f)", k=Q4, p=P)[k]).then_inc(s_el, 16)
            sp.wait_ge(s_dc, 1)
            for k, t in enumerate((rdeg_row, deg_row)):
                sp.dma_start(t.rearrange("(k c) p -> c k p", k=Q4), q(OB[0:BC, k, :])).then_inc(s_dr, 16)

            sp.wait_ge(s_dr, 32)

            def walk(ph):
                sp.wait_ge(s_rel, 1)
                with sp.Fori(0, SPINS) as i:
                    places = from_table(sp, tab_dest, i * US, US, BLOCKS + STEPS - 1)
                    for j, to in enumerate(places):
                        s = i * US + j
                        sp.wait_ge(acc_steps, s + (CREDIT + STEPS * ph + 1))
                        sp.dma_start(agg.rearrange("b f n -> f b n")[:, ds(to, 1), :].rearrange("f o n -> f (o n)"), ACC[:, j % SUMS, :]).then_inc(out_done[j % SUMS], 16)
                written(sp, ph)

            walk(0)
            with sp.Fori(0, TURNS) as i:
                for b in range(2):
                    sp.wait_ge(Z_[b], i + at(1, "z"))
                    sp.dma_start(q(IN[:, b, :]), sums(i * 2 + b)).then_inc(IN_[b], 16)
            for d, base in ((2, x_pad), (3, state)):
                walk(d - 1)
                with sp.Fori(0, TURNS) as i:
                    for b in range(2):
                        sp.wait_ge(STAT[b], i + at(d, "stat"))
                        sp.dma_start(q(IN[:, b, :]), sums(i * 2 + b)).then_inc(IN_[b], 16)
                        sp.dma_start(q(XB[:, b, :]), rows(base, i * 2 + b)).then_inc(IN_[b], 16)
            walk(3)
            def load4(i, b):
                g = 2 * i + b
                sp.wait_ge(TR[b], i + at(4, "tr"))
                sp.dma_start(q(IN[:, b, :]), sums(g)).then_inc(IN_[b], 16)
                sp.dma_start(q(HB[:, b, :]), rows(tabs[1], g)).then_inc(IN_[b], 16)
                sp.wait_ge(MMA[b], i + at(4, "mma"))
                sp.dma_start(RB[:, b, :], rdeg_row.rearrange("(g j) p -> g (j p)", j=Q4)[ds(g, 1), :].broadcast_to([P, 512])).then_inc(IN_[b], 16)

            def load4_state(i, b):
                sp.wait_ge(Z_[b], i + at(4, "z"))
                sp.dma_start(q(XB[:, b, :]), rows(state, 2 * i + b)).then_inc(LATE[b], 16)

            staggered(sp, [(0, load4), (1, load4_state)])
            stored(sp, 4)
            walk(4)
            with sp.Fori(0, TURNS) as i:
                for b in range(2):
                    sp.wait_ge(STAT[b], i + at(5, "stat"))
                    sp.dma_start(q(IN[:, b, :]), sums(2 * i + b)).then_inc(IN_[b], 16)
                    sp.dma_start(q(XB[:, b, :]), rows(state, 2 * i + b)).then_inc(IN_[b], 16)
            stored(sp, 5)
            walk(5)

            def load6(i, b):
                g = 2 * i + b
                sp.wait_ge(TR[b], i + at(6, "tr"))
                sp.dma_start(q(IN[:, b, :]), sums(g)).then_inc(IN_[b], 16)
                sp.wait_ge(ADDED[b], i + at(6, "hid"))
                sp.dma_start(q(HB[:, b, :]), rows(h5_d, g)).then_inc(IN_[b], 16)

            def load6_late(i, b):
                g = 2 * i + b
                sp.wait_ge(MMB[b], i + at(6, "mmb"))
                sp.dma_start(RB[0:1, b, :], deg_row.rearrange("(g j) p -> g (j p)", j=Q4)[ds(g, 1), :]).then_inc(LATE[b], 16)
                sp.wait_ge(SUMMED[b], i + at(6, "at"))
                sp.dma_start(q(XB[:, b, :]), rows(state, g)).then_inc(LATE[b], 16)

            staggered(sp, [(0, load6), (1, load6_late)])

        @block.gpsimd
        def _(pool):
            nc.gpsimd.memset(src_o[:], PAD_NODE).then_inc(s_pad, 1)
            nc.gpsimd.memset(dst_o[:], PAD_NODE).then_inc(s_pad, 1)
            nc.gpsimd.memset(ew_o[:], 0.0).then_inc(s_pad, 1)
            nc.gpsimd.memset(mhalf[:], -0.5)
            nc.gpsimd.memset(ones[:], 1.0).then_inc(s_const, 1)
            nc.gpsimd.memset(zero[:], 0.0).then_inc(s_const, 1)
            nc.gpsimd.iota(iota_i[:], [[1, WS]], base=0, channel_multiplier=0).then_inc(s_const, 1)
            nc.gpsimd.iota(part_i[:], [[1, 1]], base=0, channel_multiplier=1).then_inc(s_const, 1)
            pool.wait_ge(s_const, 4)
            nc.gpsimd.affine_select(out=ident[:], in_=zero[:], compare_op=ALU.not_equal, fill=1.0, base=0,
                                    pattern=[[-1, P]], channel_multiplier=1).then_inc(s_const, 1)
            nc.gpsimd.affine_select(out=upper[:], in_=zero[:], compare_op=ALU.is_ge, fill=1.0, base=0,
                                    pattern=[[-1, P]], channel_multiplier=1).then_inc(s_const, 1)
            pool.wait_ge(s_deg1, 1)
            for t in (nsrc, ndst):
                nc.gpsimd.tensor_tensor(t[:, :], t[:, :], mhalf[:, :], ALU.pow).then_inc(s_pow, 1)

            with pool.Fori(0, CHUNKS // 2) as i:
                for b in range(2):
                    pool.wait_ge(s_pack[b], i + 1)
                    stand(pool)
                    for j in range(CH):
                        nc.gpsimd.indirect_dma_start(
                            out=edges, out_offset=bass.IndirectOffsetOnAxis(ap=pos_i[b][:, j:j + 1], axis=0),
                            in_=pack[b][:, j, :], in_offset=None).then_inc(s_scat[b], 16)

            chain = Chain(pool, link_p)
            link = chain.link

            def coefficients(d, scaled=False):
                def coefs(i, b):
                    pool.wait_ge(STAT[b], i + (at(d, "stat") + 1))
                    stand(pool)
                    nc.gpsimd.tensor_scalar(NM[:, b, :], MV[:, b, :, 0], -1.0, None, ALU.mult)
                    link(nc.gpsimd.tensor_scalar(VE[:, b, :], MV[:, b, :, 1], EPS, None, ALU.add))
                    link(nc.gpsimd.tensor_tensor(SC[:, b, :], VE[:, b, :], mhalf[:, 0:Q4], ALU.pow))
                    if scaled:
                        link(nc.gpsimd.tensor_tensor(SC[:, b, :], SC[:, b, :], nsrc[:, ds(i * 2 * Q4 + b * Q4, Q4)], ALU.mult))
                    link(nc.gpsimd.tensor_tensor(BI[:, b, :], NM[:, b, :], SC[:, b, :], ALU.mult))
                    pool.sem_inc((COEF if d == 0 else Z_)[b], 1)

                def add_b2(i, b):
                    pool.wait_ge(IN_[b], i * 32 + (at(2, "in") + 32))
                    pool.wait_ge(STAT[b], i + at(2, "stat"))
                    stand(pool)
                    nc.gpsimd.tensor_tensor(XS[:, b, :], XB[:, b, :], b2x4[:, :], ALU.add).then_inc(ADDED[b], 1)

                def add_bu2(i, b):
                    pool.wait_ge(IN_[b], i * 32 + (at(6, "in") + 32))
                    pool.wait_ge(STAT[b], i + at(6, "stat"))
                    stand(pool)
                    nc.gpsimd.tensor_tensor(T1[:, b, :], HB[:, b, :], bu2x4[:, :], ALU.add).then_inc(ADDED[b], 1)

                def add_beta(i, b):
                    pool.wait_ge(LATE[b], i * 32 + (at(6, "late") + 32))
                    pool.wait_ge(OUT[b], i + at(6, "out"))
                    stand(pool)
                    nc.gpsimd.tensor_tensor(XS[:, b, :], XB[:, b, :], bet4[:, :], ALU.add).then_inc(SUMMED[b], 1)

                staggered(pool, {2: [(0, add_b2), (0, coefs)], 6: [(1, add_bu2), (2, coefs), (2, add_beta)]}.get(d, [(0, coefs)]),
                          chain, 3 + scaled)

            pool.wait_ge(s_pow, 2)
            coefficients(0, True)

            def gather(table, idx, slot, done, add):
                nc.gpsimd.indirect_dma_start(
                    out=M[:, slot, :], out_offset=None, in_=table,
                    in_offset=bass.IndirectOffsetOnAxis(ap=idx, axis=0),
                    **({"compute_op": ALU.add} if add else {})).then_inc(done, 16)

            def walk(ph, table, d):
                stored(pool, d)

                def chunk(b, ready, last):
                    pool.wait_ge(idx_ready, ready)
                    if last is not None:
                        pool.wait_ge(pe_steps, last)
                    stand(pool)
                    for j in range(CH):
                        gather(table, six[b][:, j:j + 1], b * CH + j, gathered[b * CH + j], False)

                for b in range(2):
                    chunk(b, CHUNKS * ph + b + 1, None)
                with pool.Fori(1, CHUNKS // 2) as i:
                    for b in range(2):
                        last = pool.value_load(tab_last[0:1, ds(i * 2 * CH + ((b - 1) * CH - 1), 1)], min_val=0, max_val=STEPS - 1)
                        chunk(b, i * 2 + (CHUNKS * ph + b + 1), last + (CREDIT + STEPS * ph + 1))

            walk(0, tabs[0], 0)
            walk(1, tabs[1], 1)
            coefficients(2)
            walk(2, tabs[0], 2)
            coefficients(3)
            walk(3, tabs[1], 3)
            walk(4, tabs[0], 4)
            coefficients(5)
            stored(pool, 5)
            with pool.Fori(0, CHUNKS // 2) as i:
                for b in range(2):
                    pool.wait_ge(slots_set, i * 2 + (b + 1))
                    stand(pool)
                    for j in range(CH):
                        gather(tabs[1], six[b][:, j:j + 1], b * CH + j, gathered[b * CH + j], True)
                    for j in range(CH):
                        pool.wait_ge(gathered[b * CH + j], i * 32 + 16 * (5 * (CHUNKS // 2) + 1))
                        stand(pool)
                        gather(q_tab, dix[b][:, j:j + 1], b * CH + j, gathered[b * CH + j], True)

            coefficients(6)

        @block.scalar
        def _(act):
            def relu(dst_, src_, scale, bias_=0.0, func=ACT.Relu):
                return nc.scalar.activation(dst_, src_, func, bias=bias_, scale=scale)

            def store(d, b, t, buf, g, done=ST_):
                act.dma_start(rows(t, g), q(buf[:, b, :])).then_inc(done[b], 16)

            def normed(d, src_, coef):
                def do(i, b):
                    act.wait_ge(D[coef][b], i + 1 + at(d, coef))
                    if d in (3, 5):
                        act.wait_ge(ST_[b], i * 32 + at(d, "st"))
                    if d != 3:
                        act.wait_ge(TR[b], i + at(d, "tr"))
                    stand(act)
                    for j in range(Q4):
                        last = relu(q(HO[:, b, :])[:, j, :], q(src_[:, b, :])[:, j, :], SC[:, b, j:j + 1], BI[:, b, j:j + 1])
                    last.then_inc(OUT[b], 1)
                return do

            def turned(d):
                def do(i, b):
                    act.wait_ge(TR[b], i + (at(d, "tr") + 1))
                    act.wait_ge(MM[b], i + at(d, "mm"))
                    stand(act)
                    nc.scalar.activation(HT[:, b, :], ps[b][:, :], ACT.Copy).then_inc(HT_[b], 1)
                return do

            def product(d):
                late = LSTORE if d == 5 else ST_
                def do(i, b):
                    act.wait_ge(MM[b], i + (at(d, "mm") + 1))
                    act.wait_ge(late[b], i * (32 if d == 5 else USES["st"][d]) + at(d, "mmc" if d == 5 else "st"))
                    stand(act)
                    nc.scalar.activation(T1[:, b, :], ps[2 + b][:, :], ACT.Copy).then_inc(GL[b], 1)
                    act.wait_ge(GL[b], i + (at(d, "gl") + 1))
                    store(d, b, tabs[d % 2], T1, i * 2 + b, late)
                    if d in (2, 5):
                        act.wait_ge(EV[b], i + (at(d, "ev") + 1))
                        store(d, b, state if d == 2 else q_tab, T2, i * 2 + b, late)
                return do

            staggered(act, [(0, normed(0, XB, "coef")), (1, product(0)), (0, turned(0))])

            def lists(h, b, ready):
                nc.scalar.activation(six[b][:, :], srcT[:, ds(h * CH, CH)], ACT.Copy).then_inc(ready, 1)

            def walk(ph):
                def forward(b, value):
                    for j in range(CH):
                        act.wait_ge(gathered[b * CH + j], value)
                        act.sem_inc(tiles_ready, 1)

                lists(0, 0, idx_ready)
                with act.Fori(0, CHUNKS // 2 - 1) as i:
                    for b in range(2):
                        lists(i * 2 + (b + 1), 1 - b, idx_ready)
                        forward(b, i * 16 + 16 * (CHUNKS // 2 * ph + 1))
                h = CHUNKS - 2
                lists(h + 1, 1, idx_ready)
                for b in range(2):
                    forward(b, 16 * CHUNKS // 2 * (ph + 1))

            act.wait_ge(s_rel, 1)
            act.wait_ge(s_pow, 2)
            walk(0)
            def hidden1(i, b):
                act.wait_ge(Z_[b], i + (at(1, "z") + 1))
                act.wait_ge(TR[b], i + at(1, "tr"))
                stand(act)
                for j in range(Q4):
                    last = relu(q(HO[:, b, :])[:, j, :], q(Z[:, b, :])[:, j, :], nsrc[:, ds(i * 2 * Q4 + (b * Q4 + j), 1)])
                last.then_inc(OUT[b], 1)

            staggered(act, [(0, hidden1), (1, product(1)), (0, turned(1))])
            walk(1)
            staggered(act, [(0, normed(2, Z, "z")), (1, product(2)), (0, turned(2))])
            walk(2)
            norm3 = normed(3, Z, "z")
            with act.Fori(0, TURNS) as i:
                for b in range(2):
                    norm3(i, b)
                    act.wait_ge(OUT[b], i + 1 + at(3, "out"))
                    store(3, b, tabs[1], HO, i * 2 + b)
                    store(3, b, state, Z, i * 2 + b)
            walk(3)

            def turned4(i, b):
                act.wait_ge(TR[b], i + 1 + at(4, "tr"))
                act.wait_ge(MMA[b], i + at(4, "mma"))
                stand(act)
                nc.scalar.activation(HT[:, b, :], ps[0][:, :], ACT.Copy).then_inc(HT_[b], 1)

            def hidden4(i, b):
                act.wait_ge(MMA[b], i + 1 + at(4, "mma"))
                act.wait_ge(MM[b], i + at(4, "mm"))
                stand(act)
                nc.scalar.activation(T1[:, b, :], ps[2][:, :], ACT.Relu, bias=b1col[:, 0:1])
                nc.scalar.activation(T2[:, b, :], ps[3][:, :], ACT.Relu, bias=b1col[:, 1:2]).then_inc(HID[b], 1)

            def table4(i, b):
                act.wait_ge(MM[b], i + 1 + at(4, "mm"))
                act.wait_ge(ST_[b], i * 32 + at(4, "st"))
                stand(act)
                nc.scalar.activation(HO[:, b, :], ps[4 + b][:, :], ACT.Copy).then_inc(OUT[b], 1)
                act.wait_ge(OUT[b], i + 1 + at(4, "out"))
                store(4, b, tabs[0], HO, 2 * i + b)
                act.wait_ge(Z_[b], i + 1 + at(4, "z"))
                store(4, b, state, Z, 2 * i + b)

            staggered(act, [(0, turned4), (1, hidden4), (3, table4)])
            walk(4)
            norm5 = normed(5, Z, "z")

            def normed5(i, b):
                norm5(i, b)
                act.wait_ge(OUT[b], i + 1 + at(5, "out"))
                store(5, b, h5_d, HO, 2 * i + b)
                store(5, b, state, Z, 2 * i + b)

            staggered(act, [(0, normed5), (1, product(5)), (0, turned(5))])
            stored(act, 5)
            half = CHUNKS // 2

            def prepare(h, b):
                nc.scalar.activation(six[b][:, :], srcT[:, ds(h * CH, CH)], ACT.Copy)
                nc.scalar.activation(dix[b][:, :], dstT[:, ds(h * CH, CH)], ACT.Copy)
                for j in range(CH):
                    last = nc.scalar.activation(M[:, b * CH + j, :], we1c[:, :], ACT.Copy, scale=ewT[:, ds(h * CH + j, 1)])
                last.then_inc(slots_set, 1)

            def hidden(b, value, last):
                if last is not None:
                    act.wait_ge(pe_steps, last)
                for j in range(CH):
                    act.wait_ge(gathered[b * CH + j], value)
                    stand(act)
                    nc.scalar.activation(GE[:, b * CH + j, :], M[:, b * CH + j, :], ACT.Gelu).then_inc(tiles_ready, 1)

            prepare(0, 0)
            for b in range(2):
                act.wait_ge(tiles_ready, 5 * TILES + b * CH - CH) if b else None
                prepare(b + 1, 1 - b) if b == 0 else None
                hidden(b, 80 * half + 32, None)
            act.wait_ge(tiles_ready, 5 * TILES + 2 * CH)
            prepare(2, 0)
            with act.Fori(1, half - 1) as i:
                for b in range(2):
                    last = act.value_load(tab_last[0:1, ds(i * 2 * CH + ((b - 1) * CH - 1), 1)], min_val=0, max_val=STEPS - 1)
                    act.wait_ge(tiles_ready, i * 2 * CH + (5 * TILES + b * CH))
                    stand(act)
                    prepare(i * 2 + (b + 1), 1 - b)
                    hidden(b, i * 32 + (80 * half + 32), last + (CREDIT + STEPS * 5 + 1))
            for b in range(2):
                h = CHUNKS - 2 + b
                last = act.value_load(tab_last[0:1, CH * (h - 1) - 1:CH * (h - 1)], min_val=0, max_val=STEPS - 1)
                if b == 0:
                    act.wait_ge(tiles_ready, 6 * TILES - 2 * CH)
                    prepare(CHUNKS - 1, 1)
                hidden(b, 112 * half, last + (CREDIT + STEPS * 5 + 1))
            def turned6(i, b):
                act.wait_ge(TR[b], i + 1 + at(6, "tr"))
                act.wait_ge(MMB[b], i + at(6, "mmb"))
                stand(act)
                nc.scalar.activation(HT[:, b, :], ps[0][:, :], ACT.Copy)
                nc.scalar.activation(AG[:, b, :], ps[1][:, :], ACT.Copy).then_inc(HT_[b], 1)

            def hidden6(i, b):
                act.wait_ge(MMB[b], i + 1 + at(6, "mmb"))
                act.wait_ge(MMC[b], i + at(6, "mmc"))
                stand(act)
                nc.scalar.activation(T2[:, b, :], ps[4 + b][:, :], ACT.Gelu, bias=bu1col[:, 0:1]).then_inc(GL[b], 1)

            def normed6(i, b):
                act.wait_ge(Z_[b], i + 1 + at(6, "z"))
                act.wait_ge(OUT[b], i + at(6, "out"))
                stand(act)
                for j in range(Q4):
                    last = nc.scalar.activation(q(HO[:, b, :])[:, j, :], q(Z[:, b, :])[:, j, :], ACT.Identity,
                                                scale=SC[:, b, j:j + 1], bias=BI[:, b, j:j + 1])
                last.then_inc(NRM[b], 1)

            def store6(i, b):
                act.wait_ge(OUT[b], i + 1 + at(6, "out"))
                g = i * 2 + b
                if not isinstance(g, int) or g < GROUPS - 1:
                    rows_out = out[0:(GROUPS - 1) * 512].rearrange("(g j p) d -> g p j d", j=Q4, p=P)
                    act.dma_start(rows_out[g], q(OB[:, b, :])).then_inc(ST_[b], 16)
                    return
                r0 = (GROUPS - 1) * 512
                nb, rest = divmod(NODES - r0, P)
                act.dma_start(out[r0:r0 + nb * P].rearrange("(j p) d -> p j d", p=P),
                              q(OB[:, b, :])[:, 0:nb, :]).then_inc(ST_[b], 16)
                act.dma_start(out[r0 + nb * P:NODES], q(OB[:, b, :])[0:rest, nb, :]).then_inc(ST_[b], 16)

            staggered(act, [(4, store6), (0, turned6), (1, hidden6), (3, normed6)])
            act.wait_ge(ST_[0], 16 * TURNS + at(6, "st"))
            act.wait_ge(ST_[1], 16 * (TURNS + 1) + at(6, "st"))

        @block.tensor
        def _(pe):
            mm = nc.tensor.matmul
            pe.sem_inc(pe_steps, CREDIT)
            pe.wait_ge(s_cv, 4)
            pe.wait_ge(s_w, 16 * NLOADS)
            for h in range(2):
                last = nc.tensor.transpose(ps[6][:, h * P:(h + 1) * P], wl[:, h * P:(h + 1) * P], ident[:, :])
            nc.tensor.transpose(ps[6][:, 2 * P:3 * P], we2[:, :], ident[:, :]).then_inc(s_wt, 1)
            pe.wait_ge(s_wt, 2)
            mm(ps[7][:, 0:P], we2T[:, :], wu1[:, 1, :], start=True, stop=True)
            mm(ps[7][0:1, P:2 * P], be2col[:, :], wu1[:, 1, :], start=True, stop=True).then_inc(s_wt, 1)
            for k in range(2):
                last = mm(ps[k][:, 0:BLOCKS], zero_h[:, :], oh_bk[:, 0, :], start=True, stop=False, skip_group_check=True)
            with pe.Fori(0, TILES // 2) as i:
                for c in range(2):
                    pe.wait_ge(s_oh, i * 2 + (c + 1))
                    for k in range(2):
                        last = mm(ps[k][:, 0:BLOCKS], oh_lo[:, 2 * c + k, :], oh_hi[:, 2 * c + k, :],
                                  start=False, stop=False, skip_group_check=True)
                    last.then_inc(s_hist, 1)
            pe.wait_ge(s_deg, 1)
            for k in range(Q4):
                last = mm(ps[2][0:BC, k:k + 1], deg[:, k * BC:(k + 1) * BC], ones[:, 0:1], start=True, stop=True)
            last.then_inc(s_cnt, 1)
            pe.wait_ge(s_cntc, 1)
            mm(ps[3][0:BC, 0:Q4], upper[0:BC, 0:BC], cnt[:, :], start=True, stop=False)
            mm(ps[3][0:BC, 0:Q4], ones[0:BC, 0:BC], cum[:, :], start=False, stop=True).then_inc(s_cum, 1)
            pe.wait_ge(s_diag, 1)
            for k in range(2):
                for c in range(Q4):
                    last = mm(ps[4 + k][:, c * BC:(c + 1) * BC], ones[0:BC, :], diag[:, c, :],
                              start=(c == 0), stop=False, skip_group_check=True)
            last.then_inc(s_base, 1)
            with pe.Fori(0, TILES // (2 * CH)) as i:
                for c in range(2 * CH):
                    bank = ps[4 + c % 2][:, 0:BLOCKS]
                    pe.wait_ge(s_rk, i * 2 * CH + (c + 1))
                    pe.wait_ge(s_rr, i * 2 * CH + (c + 1))
                    mm(bank, ones_h[:, :], oh_bk[:, (c - 1) % CH, :], start=False, stop=False, skip_group_check=True)
                    mm(bank, lower_h[:, :], oh_bk[:, (c - 2) % CH, :], start=False, stop=False, skip_group_check=True)
                    mm(bank, upper_h[:, :], oh_bk[:, c % CH, :], start=False, stop=False, skip_group_check=True).then_inc(s_rank, 1)
            n = 0
            for kind in range(5):
                w = TABW[kind]
                if kind >= 2:
                    pe.wait_ge(s_tabr, kind - 1)
                for c in range(Q4):
                    pe.wait_ge(s_ge, n + 1)
                    n += 1
                    last = mm(ps[2 + kind % 2][:, 0:w], ones[0:BC, :], ge[:, 0:w], start=(c == 0), stop=(c == Q4 - 1))
                    last.then_inc(s_tabm, 1)
            for k, t in enumerate((rdeg, deg)):
                for c in range(Q4):
                    last = nc.tensor.transpose(ps[k][0:BC, c * P:(c + 1) * P], t[:, c * BC:(c + 1) * BC], ident[:, :])
            last.then_inc(s_dt, 1)
            def block_products(bank, lhs, w):
                for j in range(Q4):
                    last = mm(q(bank[:, :])[:, j, :], lhs[:, j, :], w, start=True, stop=True)
                return last

            def turn_rows(bank, src_):
                for j in range(Q4):
                    last = nc.tensor.transpose(q(bank[:, :])[:, j, :], src_[:, j, :], ident[:, :])
                return last

            def dense_table(d, w):
                with pe.Fori(0, TURNS) as i:
                    for b in range(2):
                        pe.wait_ge(OUT[b], i + (at(d, "out") + 1))
                        pe.wait_ge(HT_[b], i + at(d, "ht"))
                        turn_rows(ps[b], q(HO[:, b, :])).then_inc(TR[b], 1)
                        pe.wait_ge(HT_[b], i + (at(d, "ht") + 1))
                        pe.wait_ge(GL[b], i + at(d, "gl"))
                        if d < 2:
                            block_products(ps[2 + b], q(HT[:, b, :]), w).then_inc(MM[b], 1)
                            continue
                        pe.wait_ge(EV[b], i + at(d, "ev"))
                        for j in range(Q4):
                            mm(q(ps[2 + b][:, :])[:, j, :], q(HT[:, b, :])[:, j, :], w[:, 0, :], start=True, stop=True)
                            o = q(ps[4 + b][:, :])[:, j, :]
                            last = mm(o, q(HT[:, b, :])[:, j, :], w[:, 1, :], start=True, stop=(d == 5))
                            if d == 2:
                                last = mm(o, ones[0:1, :], linb[:, :], start=False, stop=True)
                        last.then_inc(MM[b], 1)

            pe.wait_ge(s_dc, 1)
            dense_table(0, w1[:, :])
            for n in range(3 * Q4):
                pe.wait_ge(s_ec, n + 1)
                if n >= 2:
                    pe.wait_ge(s_er, n - 1)
                k, c = divmod(n, Q4)
                nc.tensor.transpose(ps[6 + n % 2][:, 0:BC], e_f[:, :], ident[0:BC, 0:BC]).then_inc(s_et, 1)

            def walk(ph):
                pe.wait_ge(s_rel, 1)
                with pe.Fori(0, SPINS) as i:
                    for j, t in enumerate(from_table(pe, tab_t, i * US, US, TILES - 1)):
                        s = i * US + j
                        slot = t % RING
                        ring = GE if ph == 5 else M
                        rows_ = ring[:, ds(slot, 1), :].rearrange("p o d -> p (o d)")
                        pe.wait_ge(tiles_ready, t + (TILES * ph + 1))
                        pe.wait_ge(oh_done, s + (WS * ph + 1))
                        pe.wait_ge(acc_steps, s + (CREDIT + STEPS * ph - 2))
                        mm(ps[j % 3][:, 0:P], OH[:, j % 3, :], rows_, start=True, stop=True).then_inc(pe_steps, 1)

            walk(0)
            dense_table(1, w2[:, :])
            walk(1)
            dense_table(2, wlT)
            walk(2)
            walk(3)
            def turn4(i, b):
                pe.wait_ge(IN_[b], i * 48 + (48 + at(4, "in")))
                pe.wait_ge(HT_[1 - b], i + b + at(4, "ht"))
                pe.wait_ge(MEAN[1 - b], i + b + at(4, "mean"))
                turn_rows(ps[0], q(HB[:, b, :]))
                turn_rows(ps[1], q(IN[:, b, :])).then_inc(TR[b], 1)

            def hidden4(i, b):
                pe.wait_ge(HT_[b], i + 1 + at(4, "ht"))
                pe.wait_ge(MEAN[b], i + 1 + at(4, "mean"))
                pe.wait_ge(HID[1 - b], i + b + at(4, "hid"))
                for h in range(2):
                    mm(ps[2 + h][:, :], ws1[:, h * P:(h + 1) * P], HT[:, b, :], start=True, stop=False)
                    last = mm(ps[2 + h][:, :], wn1[:, h * P:(h + 1) * P], RB[:, b, :], start=False, stop=True)
                last.then_inc(MMA[b], 1)

            def out4(i, b):
                pe.wait_ge(HID[b], i + 1 + at(4, "hid"))
                pe.wait_ge(OUT[b], i + at(4, "out"))
                pe.wait_ge(Z_[b], i + at(4, "z"))
                for j in range(Q4):
                    for k in range(2):
                        o = q(ps[4 + 2 * k + b][:, :])[:, j, :]
                        for h, t in enumerate((T1, T2)):
                            last = mm(o, q(t[:, b, :])[:, j, :], w42[:, h, k, :], start=(h == 0), stop=(h == 1))
                last.then_inc(MM[b], 1)

            staggered(pe, [(0, turn4), (1, hidden4), (2, out4)])
            walk(4)
            dense_table(5, we1)
            walk(5)

            def turn6(i, b):
                pe.wait_ge(IN_[b], i * 32 + (32 + at(6, "in")))
                pe.wait_ge(HT_[1 - b], i + b + at(6, "ht"))
                turn_rows(ps[0], q(HB[:, b, :]))
                turn_rows(ps[1], q(IN[:, b, :])).then_inc(TR[b], 1)

            def hidden6(i, b):
                pe.wait_ge(HT_[b], i + 1 + at(6, "ht"))
                pe.wait_ge(LATE[b], i * 32 + (32 + at(6, "late")))
                pe.wait_ge(GL[b], i + at(6, "gl"))
                mm(ps[4 + b][:, :], wu1[:, 0, :], HT[:, b, :], start=True, stop=False)
                mm(ps[4 + b][:, :], wm[:, :], AG[:, b, :], start=False, stop=False)
                mm(ps[4 + b][:, :], cm[:, :], RB[0:1, b, :], start=False, stop=True).then_inc(MMB[b], 1)

            def out6(i, b):
                pe.wait_ge(GL[b], i + 1 + at(6, "gl"))
                pe.wait_ge(Z_[b], i + at(6, "z"))
                block_products(ps[6 + b], q(T2[:, b, :]), wu2[:, :]).then_inc(MMC[b], 1)

            staggered(pe, [(0, turn6), (1, hidden6), (2, out6)])

        @block.vector
        def _(dve):
            v = nc.vector
            chain = Chain(dve, link_v)
            link = chain.link
            v.memset(oh_bk[:], 0.0)
            v.memset(dhi[:, TILES:TILES + 1], 0.0)
            for k in range(2):
                v.memset(pack[k][:], 0)
            dve.sem_inc(acc_steps, CREDIT)
            dve.wait_ge(s_const, 6)
            v.tensor_copy(iota_f[:], iota_i[:]).then_inc(s_cv, 1)
            v.tensor_copy(iota_h[:], iota_i[:, 0:BLOCKS]).then_inc(s_cv, 1)
            v.tensor_copy(part_f[:], part_i[:])
            v.tensor_copy(upper_h[:], upper[:])
            v.tensor_copy(ones_h[:], ones[:])
            link(v.memset(zero_h[:], 0.0))
            v.tensor_tensor(lower_h[:], ones_h[:], upper_h[:], ALU.subtract).then_inc(s_cv, 1)
            dve.wait_ge(s_cv, 3)
            dve.wait_ge(s_load, 96)
            for t, lo, hi in ((src_o, slo, shi), (dst_o, dlo, dhi)):
                link(v.tensor_scalar(cut_i[:], t[:], P - 1, None, ALU.bitwise_and))
                link(v.tensor_copy(lo[:], cut_i[:]))
                link(v.tensor_scalar(cut_i[:], t[:], 7, None, ALU.logical_shift_right))
                link(v.tensor_copy(hi[:, 0:TILES], cut_i[:]))
            dve.wait_ge(s_w, 16 * NLOADS)
            dve.sem_inc(s_cv, 1)
            dve.wait_ge(s_wt, 1)
            v.tensor_copy(wlT[:, 0, :], ps[6][:, P:2 * P])
            v.tensor_copy(wlT[:, 1, :], ps[6][:, 0:P])
            v.tensor_copy(we2T[:, :], ps[6][:, 2 * P:3 * P]).then_inc(s_wt, 1)
            dve.wait_ge(s_wt, 3)
            v.tensor_copy(wm[:, :], ps[7][:, 0:P])
            v.tensor_copy(cm[:, :], ps[7][0:1, P:2 * P])
            for t4, t in ((b2x4, b2bc), (gam4, gam), (bet4, bet), (sb2x4, sb2bc), (be1x4, be1bc), (bu2x4, bu2bc)):
                for j in range(Q4):
                    last = v.tensor_copy(q(t4[:, :])[:, j, :], t[:, :])
            link(last)


            def hist_column(i, c, wait):
                if wait is not None:
                    dve.wait_ge(s_hist, wait)
                col = i * 2 + c
                for k, (lo, hi) in enumerate(((slo, shi), (dlo, dhi))):
                    v.tensor_scalar(oh_lo[:, 2 * c + k, :], iota_h[:, 0:P], lo[:, ds(col, 1)], None, ALU.is_equal)
                    last = v.tensor_scalar(oh_hi[:, 2 * c + k, :], iota_h[:, :], hi[:, ds(col, 1)], None, ALU.is_equal)
                last.then_inc(s_oh, 1)

            hist_column(0, 0, None)
            hist_column(0, 1, None)
            with dve.Fori(1, TILES // 2) as i:
                for c in range(2):
                    hist_column(i, c, i * 2 + (c - 1))
            dve.wait_ge(s_hist, TILES)
            v.tensor_copy(deg[:, :], ps[1][:, 0:BLOCKS]).then_inc(s_deg, 1)
            link(v.tensor_scalar(nsrc[:, :], ps[0][:, 0:BLOCKS], 1.0, None, ALU.max))
            link(v.tensor_scalar(ndst[:, :], deg[:, :], 1.0, None, ALU.max))
            link(v.reciprocal(rdeg[:, :], ndst[:, :]))
            dve.sem_inc(s_deg1, 1)
            dve.wait_ge(s_cnt, 1)
            link(v.tensor_copy(cnt[:, :], ps[2][0:BC, 0:Q4]))
            link(v.memset(cum[:, 0:1], 0.0))
            for k in range(1, Q4):
                link(v.tensor_tensor(cum[:, k:k + 1], cum[:, k - 1:k], cnt[:, k - 1:k], ALU.add))
            dve.sem_inc(s_cntc, 1)
            dve.wait_ge(s_cum, 1)
            link(v.tensor_copy(before[:, :], ps[3][0:BC, 0:Q4]))
            for k in range(Q4):
                last = v.tensor_scalar(diag[:, k, :], ident[0:BC, 0:BC], before[:, k:k + 1], None, ALU.mult)
            last.then_inc(s_diag, 1)
            link(v.tensor_copy(before_i[:, :], before[:, :]))
            link(v.tensor_scalar(before_i[:, :], before_i[:, :], 7, None, ALU.logical_shift_right))
            link(v.tensor_copy(first[:, :], before_i[:, :]))
            for k in range(Q4):
                link(v.tensor_scalar(blk[:, k:k + 1], part_f[0:BC, :], float(k * BC), None, ALU.add))
            link(v.tensor_tensor(start[:, :], first[:, :], blk[:, :], ALU.add))

            def rank_onehot(col, c):
                v.tensor_scalar(oh_bk[:, c % CH, :], iota_h[:, :], dhi[:, ds(col, 1)], None, ALU.is_equal).then_inc(s_rk, 1)

            rank_onehot(0, 0)
            dve.sem_inc(s_rr, 2)
            with dve.Fori(0, TILES // (2 * CH)) as i:
                for c in range(2 * CH):
                    b = c // CH
                    rank_onehot(i * 2 * CH + (c + 1), c + 1)
                    dve.wait_ge(s_rank, i * 2 * CH + (c + 1))
                    v.tensor_tensor_reduce(junk[:, c % 2, :], ps[4 + c % 2][:, 0:BLOCKS], oh_bk[:, c % CH, :], 1.0, 0.0,
                                           ALU.mult, ALU.add, posf[:, c:c + 1]).then_inc(s_rr, 1)
                    if c % CH == CH - 1:
                        dve.wait_ge(s_rr, i * 2 * CH + (c + 1 + 2))
                        dve.wait_ge(s_scat[b], i * (16 * CH))
                        stand(dve)
                        for f, t in enumerate((src_o[:, :], dst_o[:, :], ew_o[:, :].bitcast(I32))):
                            v.tensor_copy(pack[b][:, :, f], t[:, ds(i * 2 * CH + b * CH, CH)])
                        v.tensor_copy(pos_i[b][:, :], posf[:, b * CH:(b + 1) * CH]).then_inc(s_pack[b], 1)

            n = 0
            for kind in range(5):
                lo = 512 * (kind % 2) if kind < 4 else 0
                for c in range(Q4):
                    if n:
                        dve.wait_ge(s_tabm, n)
                    n += 1
                    col = (first if kind == 4 else start)[:, c:c + 1]
                    v.tensor_scalar(ge[:, 0:TABW[kind]], iota_f[0:BC, lo:lo + TABW[kind]], col, None,
                                    ALU.is_equal if kind in (2, 3) else ALU.is_ge).then_inc(s_ge, 1)
                dve.wait_ge(s_tabm, n)
                got = ps[2 + kind % 2]
                if kind < 2:
                    ins = v.tensor_scalar(b_row[:, lo:lo + TABW[kind]], got[:, 0:TABW[kind]], -1.0, None, ALU.add)
                elif kind < 4:
                    ins = v.tensor_scalar(keep[:, lo:lo + TABW[kind]], got[:, 0:TABW[kind]], -1.0, 1.0, ALU.mult, ALU.add)
                else:
                    ins = v.scalar_tensor_tensor(ls_row[:, :], got[0:1, 0:TILES], -1.0, iota_f[0:1, 0:TILES], ALU.add, ALU.add)
                chain.link(ins)
                dve.sem_inc(s_tabr, 1)
            link(v.memset(keep[:, STEPS:STEPS + 1], 0.0))
            link(v.tensor_tensor(t_row[:, :], iota_f[0:1, :], b_row[0:1, :], ALU.subtract))
            link(v.scalar_tensor_tensor(dest_f[:, 0:STEPS], t_row[:, 0:STEPS], float(BLOCKS), keep[0:1, 1:STEPS + 1], ALU.add, ALU.mult))
            link(v.tensor_tensor(dest_f[:, 0:STEPS], dest_f[:, 0:STEPS], b_row[0:1, 0:STEPS], ALU.add))
            v.tensor_copy(tab_t[:, 0:STEPS], t_row[:, 0:STEPS])
            v.tensor_copy(tab_dest[:, 0:STEPS], dest_f[:, 0:STEPS])
            link(v.tensor_copy(tab_last[:, :], ls_row[:, :]))
            link(v.tensor_scalar(b_row[:, :], b_row[:, :], float(P), None, ALU.mult))
            dve.wait_ge(s_dt, 1)
            for k in range(2):
                last = v.tensor_copy(OB[0:BC, k, :], ps[k][0:BC, :])
            last.then_inc(s_dc, 1)

            def norm(b, src_):
                for j in range(Q4):
                    last = v.bn_stats(ST[:, b, j, :], src_[:, j, :])
                link(last)
                stand(dve)
                for j in range(Q4):
                    last = v.bn_aggr(MV[:, b, j, :], ST[:, b, j, :])
                return last

            with dve.Fori(0, TURNS) as i:
                chain.turn(i, 2 * 1)
                for b in range(2):
                    dve.wait_ge(IN_[b], i * 16 + 16 + at(0, "in"))
                    dve.wait_ge(OUT[b], i + at(0, "out"))
                    norm(b, q(XB[:, b, :])).then_inc(STAT[b], 1)
                chain.over(TURNS)

            dve.wait_ge(s_el, 64)
            for n in range(3 * Q4):
                k, c = divmod(n, Q4)
                part = slice(c * BC, (c + 1) * BC)
                if n:
                    dve.wait_ge(s_et, n)
                field = e_in[:, c, :].rearrange("t (p f) -> t p f", f=4)[:, :, k]
                v.tensor_copy(e_f[:, :], field.bitcast(F32) if k == 2 else field).then_inc(s_ec, 1)
                dve.wait_ge(s_et, n + 1)
                got = ps[6 + n % 2][:, 0:BC]
                if k == 0:
                    v.tensor_copy(srcT[:, part], got).then_inc(s_er, 1)
                elif k == 1:
                    v.tensor_copy(dstT[:, part], got)
                    v.tensor_copy(dstF[:, part], got).then_inc(s_er, 1)
                else:
                    v.tensor_copy(ewT[:, part], got).then_inc(s_er, 1)
            dve.wait_ge(s_er, 3 * Q4)
            link(v.memset(dstrel[:, STEPS:WS], -1.0))
            with dve.Fori(0, SPINS) as i:
                for j, t in enumerate(from_table(dve, tab_t, i * US, US, TILES - 1)):
                    v.tensor_tensor(dstrel[:, ds(i * US + j, 1)], dstF[:, ds(t, 1)], b_row[:, ds(i * US + j, 1)], ALU.subtract)
            link(v.memset(ACC[:, :, :], 0.0))
            dve.sem_inc(s_rel, 1)

            def walk(ph):
                def onehot(s, k):
                    dve.wait_ge(pe_steps, s + (CREDIT + STEPS * ph - 2))
                    v.tensor_scalar(OH[:, k % 3, :], iota_f[:, 0:P], dstrel[:, ds(s, 1)], None, ALU.is_equal).then_inc(oh_done, 1)

                for k in range(LEAD):
                    onehot(k, k)
                with dve.Fori(0, SPINS) as i:
                    for j in range(US):
                        s = i * US + j
                        onehot(i * US + (j + LEAD), j + LEAD)
                        dve.wait_ge(pe_steps, s + (CREDIT + STEPS * ph + 1))
                        dve.wait_ge(acc_steps, s + (CREDIT + STEPS * ph))
                        dve.wait_ge(out_done[j % SUMS], i * (16 * US // SUMS) + (16 * LAPS * ph + 16 * (j // SUMS)))
                        v.scalar_tensor_tensor(ACC[:, j % SUMS, :], ACC[:, (j - 1) % SUMS, :], keep[:, ds(s, 1)], ps[j % 3][:, 0:P],
                                               ALU.mult, ALU.add).then_inc(acc_steps, 1)

            def per_block(b, bank, scale, other, i):
                for j in range(Q4):
                    last = v.scalar_tensor_tensor(q(Z[:, b, :])[:, j, :], q(bank)[:, j, :],
                                                  scale[:, ds((i * 2 + b) * Q4 + j, 1)], other(j), ALU.mult, ALU.add)
                return last

            dve.wait_ge(s_pow, 2)
            walk(0)
            with dve.Fori(0, TURNS) as i:
                for b in range(2):
                    dve.wait_ge(IN_[b], i * 16 + (at(1, "in") + 16))
                    dve.wait_ge(OUT[b], i + at(1, "out"))
                    per_block(b, IN[:, b, :], ndst, lambda j: b1bc[:, :], i).then_inc(Z_[b], 1)
            walk(1)
            def state2(i, b):
                dve.wait_ge(IN_[b], i * 32 + (at(2, "in") + 32))
                dve.wait_ge(ADDED[b], i + (at(2, "hid") + 1))
                dve.wait_ge(OUT[b], i + at(2, "out"))
                link(per_block(b, IN[:, b, :], ndst, lambda j: q(XS[:, b, :])[:, j, :], i))
                norm(b, q(Z[:, b, :])).then_inc(STAT[b], 1)

            def self2(i, b):
                dve.wait_ge(MM[b], i + (at(2, "mm") + 1))
                dve.wait_ge(ST_[b], i * 32 + at(2, "st"))
                stand(dve)
                link(v.tensor_tensor(T2[:, b, :], ps[4 + b][:, :], Z[:, b, :], ALU.add))
                dve.sem_inc(EV[b], 1)

            staggered(dve, [(2, self2), (0, state2)], chain, 3)
            walk(2)
            with dve.Fori(0, TURNS) as i:
                chain.turn(i, 2 * 2)
                for b in range(2):
                    dve.wait_ge(IN_[b], i * 32 + (at(3, "in") + 32))
                    dve.wait_ge(OUT[b], i + at(3, "out"))
                    dve.wait_ge(ST_[b], i * 32 + at(3, "st"))
                    link(per_block(b, IN[:, b, :], rdeg, lambda j: q(XB[:, b, :])[:, j, :], i))
                    norm(b, q(Z[:, b, :])).then_inc(STAT[b], 1)
                chain.over(TURNS)
            walk(3)
            def mean4(i, b):
                dve.wait_ge(TR[b], i + (at(4, "tr") + 1))
                dve.wait_ge(IN_[b], i * 48 + (at(4, "in") + 48))
                v.tensor_tensor(RB[:, b, :], ps[1][:, :], RB[:, b, :], ALU.mult).then_inc(MEAN[b], 1)

            def state4(i, b):
                dve.wait_ge(LATE[b], i * 16 + (16 + at(4, "late")))
                dve.wait_ge(MM[b], i + (1 + at(4, "mm")))
                dve.wait_ge(ST_[b], i * 32 + at(4, "st"))
                link(v.tensor_tensor(Z[:, b, :], ps[6 + b][:, :], XB[:, b, :], ALU.add))
                v.tensor_tensor(Z[:, b, :], Z[:, b, :], sb2x4[:, :], ALU.add).then_inc(Z_[b], 1)

            staggered(dve, [(0, mean4), (3, state4)], chain, 1)
            walk(4)

            def state5(i, b):
                dve.wait_ge(IN_[b], i * 32 + (32 + at(5, "in")))
                dve.wait_ge(OUT[b], i + at(5, "out"))
                dve.wait_ge(ST_[b], i * 32 + at(5, "st"))
                link(per_block(b, IN[:, b, :], rdeg, lambda j: q(XB[:, b, :])[:, j, :], i))
                norm(b, q(Z[:, b, :])).then_inc(STAT[b], 1)

            def dst_half(i, b):
                dve.wait_ge(MM[b], i + (1 + at(5, "mm")))
                dve.wait_ge(LSTORE[b], i * 32 + at(5, "mmc"))
                v.tensor_tensor(T2[:, b, :], ps[4 + b][:, :], be1x4[:, :], ALU.add).then_inc(EV[b], 1)

            staggered(dve, [(2, dst_half), (0, state5)], chain, 2)
            walk(5)

            def updated6(i, b):
                dve.wait_ge(ADDED[b], i + (1 + at(6, "hid")))
                dve.wait_ge(MMC[b], i + (1 + at(6, "mmc")))
                dve.wait_ge(NRM[b], i + at(6, "nrm"))
                link(v.tensor_tensor(Z[:, b, :], T1[:, b, :], ps[6 + b][:, :], ALU.add))
                norm(b, q(Z[:, b, :])).then_inc(STAT[b], 1)

            def out6(i, b):
                dve.wait_ge(NRM[b], i + (1 + at(6, "nrm")))
                dve.wait_ge(SUMMED[b], i + (1 + at(6, "at")))
                dve.wait_ge(ST_[b], i * 16 + at(6, "st"))
                link(v.tensor_tensor(OB[:, b, :], HO[:, b, :], gam4[:, :], ALU.mult))
                link(v.tensor_tensor(OB[:, b, :], OB[:, b, :], XS[:, b, :], ALU.add))
                dve.sem_inc(OUT[b], 1)

            staggered(dve, [(2, updated6), (3, out6)], chain, 4)


_INS = ["x", "src", "dst", "edge_weight", "L0_gnn_W1", "L0_gnn_b1", "L0_gnn_W2", "L0_gnn_b2", "L1_gnn_W",
        "L1_gnn_b", "L2_gnn_W_self1", "L2_gnn_W_neigh1", "L2_gnn_b1", "L2_gnn_W_self2", "L2_gnn_W_neigh2",
        "L2_gnn_b2", "L3_gnn_We1", "L3_gnn_be1", "L3_gnn_We2", "L3_gnn_be2", "L3_gnn_Wu1", "L3_gnn_bu1",
        "L3_gnn_Wu2", "L3_gnn_bu2", "L3_gnn_gamma", "L3_gnn_beta"]


def kernel(**inputs):
    import numpy as _np
    import concourse.bacc as _bacc
    from concourse.bass_utils import run_bass_kernel_spmd as _run

    nc = _bacc.Bacc("TRN2", target_bir_lowering=False, num_devices=1)
    arrays, args = {}, {}
    for name in _INS:
        arr = _np.ascontiguousarray(inputs[name])
        arrays[f"in_{name}"] = arr
        args[name] = nc.dram_tensor(f"in_{name}", arr.shape, mybir.dt.from_np(arr.dtype), kind="ExternalInput").ap()
    out = nc.dram_tensor("out_0", (NODES, P), F32, kind="ExternalOutput").ap()
    program(nc, args, out)
    r = _run(nc, [arrays], core_ids=[0])
    return r.results[0]["out_0"]
```
